# Optimizing a Trainium2 kernel written in Bass

```python
import numpy as np
import jax
import jax.numpy as jnp

def _softmax(x, axis=-1):
    return jax.nn.softmax(x, axis=axis)

def _gelu(x):
    return jax.nn.gelu(x, approximate=True)

def _silu(x):
    return jax.nn.silu(x)

def _sigmoid(x):
    return jax.nn.sigmoid(x)

def _layernorm(x, axis=-1, eps=1e-05):
    m = jnp.mean(x, axis=axis, keepdims=True)
    v = jnp.var(x, axis=axis, keepdims=True)
    return (x - m) / jnp.sqrt(v + eps)

def _scatter_add(tgt, idx, src, axis=0):
    return tgt.at[idx].add(src)

def _segment_sum(src, seg, n):
    return jax.ops.segment_sum(src, seg, n)
kernel_name = 'mk_macaron_d1_jaxref_r8_73753b'

def setup_inputs(seed: int=0):
    np.random.seed(seed)
    _w = jnp.asarray

    def _L0_attn_setup():
        import jax, jax.numpy as jnp
        import numpy as np
        D_MODEL = 128
        N_HEADS = 16
        HEAD_DIM = D_MODEL // N_HEADS

        def alibi_slopes(n_heads):
            base = 2.0 ** (-8.0 / n_heads)
            return jnp.asarray([base ** i for i in range(1, n_heads + 1)], dtype=jnp.float32)
        key = jax.random.key(seed)
        kx, kq, kk, kv, ko = jax.random.split(key, 5)
        B, T = (2, 256)
        scale = 0.02
        x = jax.random.normal(kx, (B, T, D_MODEL), dtype=jnp.float32)
        Wq = jax.random.normal(kq, (D_MODEL, D_MODEL), dtype=jnp.float32) * scale
        Wk = jax.random.normal(kk, (D_MODEL, D_MODEL), dtype=jnp.float32) * scale
        Wv = jax.random.normal(kv, (D_MODEL, D_MODEL), dtype=jnp.float32) * scale
        Wo = jax.random.normal(ko, (D_MODEL, D_MODEL), dtype=jnp.float32) * scale
        return {'x': x, 'Wq': Wq, 'Wk': Wk, 'Wv': Wv, 'Wo': Wo}
    _L0_attn_in = _L0_attn_setup()

    def _L0_ffn_setup():
        import jax, jax.numpy as jnp
        import numpy as np
        B, S, D, E, F = (2, 256, 128, 8, 512)
        key = jax.random.key(seed)
        ks = jax.random.split(key, 4)
        return {'hidden_states': jax.random.normal(ks[0], (B, S, D), dtype=jnp.float32), 'Wr': jax.random.normal(ks[1], (D, E), dtype=jnp.float32) * (1.0 / np.sqrt(D)), 'W1': jax.random.normal(ks[2], (E, D, F), dtype=jnp.float32) * (1.0 / np.sqrt(D)), 'b1': jnp.zeros((E, F), dtype=jnp.float32), 'W2': jax.random.normal(ks[3], (E, F, D), dtype=jnp.float32) * (1.0 / np.sqrt(F)), 'b2': jnp.zeros((E, D), dtype=jnp.float32)}
    _L0_ffn_in = _L0_ffn_setup()
    _d = {'L0_attn_x': _L0_attn_in['x'], 'L0_attn_Wq': _L0_attn_in['Wq'], 'L0_attn_Wk': _L0_attn_in['Wk'], 'L0_attn_Wv': _L0_attn_in['Wv'], 'L0_attn_Wo': _L0_attn_in['Wo'], 'L0_ffn_Wr': _L0_ffn_in['Wr'], 'L0_ffn_W1': _L0_ffn_in['W1'], 'L0_ffn_b1': _L0_ffn_in['b1'], 'L0_ffn_W2': _L0_ffn_in['W2'], 'L0_ffn_b2': _L0_ffn_in['b2']}
    _x0 = _d['L0_attn_x']
    _d['L0_attn_x'] = jax.random.normal(jax.random.fold_in(jax.random.key(seed), 1), (16, 256, 128), dtype=_x0.dtype)
    del _x0
    return _d

def reference(L0_attn_x, L0_attn_Wq, L0_attn_Wk, L0_attn_Wv, L0_attn_Wo, L0_ffn_Wr, L0_ffn_W1, L0_ffn_b1, L0_ffn_W2, L0_ffn_b2):

    def _L0_attn_ref(x, Wq, Wk, Wv, Wo):
        import jax, jax.numpy as jnp
        import numpy as np
        D_MODEL = 128
        N_HEADS = 16
        HEAD_DIM = D_MODEL // N_HEADS

        def alibi_slopes(n_heads):
            base = 2.0 ** (-8.0 / n_heads)
            return jnp.asarray([base ** i for i in range(1, n_heads + 1)], dtype=jnp.float32)
        B, T, D = x.shape
        H, hd = (N_HEADS, HEAD_DIM)

        def proj(W):
            return (x @ W.T).reshape(B, T, H, hd).transpose(0, 2, 1, 3)
        q, k, v = (proj(Wq), proj(Wk), proj(Wv))
        scale = hd ** (-0.5)
        scores = jnp.einsum('bhqd,bhkd->bhqk', q, k) * scale
        pos = jnp.arange(T, dtype=jnp.float32)
        dist = jnp.abs(pos[:, None] - pos[None, :])
        causal = pos[:, None] >= pos[None, :]
        slopes = alibi_slopes(H)
        bias = -slopes[:, None, None] * jnp.where(causal, dist, 0.0)
        scores = scores + bias[None]
        scores = jnp.where(causal[None, None], scores, -jnp.inf)
        attn = jax.nn.softmax(scores, axis=-1)
        out = jnp.einsum('bhqk,bhkd->bhqd', attn, v)
        out = out.transpose(0, 2, 1, 3).reshape(B, T, D)
        return out @ Wo.T

    def _L0_ffn_ref(hidden_states, Wr, W1, b1, W2, b2):
        import jax, jax.numpy as jnp
        import numpy as np
        B, S, D, E, F = (2, 256, 128, 8, 512)
        b, s, d = hidden_states.shape
        e = Wr.shape[1]
        x = hidden_states.reshape(b * s, d)
        router_logits = x @ Wr
        router_probs = jax.nn.softmax(router_logits, axis=-1)
        expert_idx = jnp.argmax(router_probs, axis=-1)
        p_max = jnp.max(router_probs, axis=-1, keepdims=True)

        def expert_mlp(w1, bb1, w2, bb2):
            h = jax.nn.gelu(x @ w1 + bb1, approximate=False)
            return h @ w2 + bb2
        outs = jax.vmap(expert_mlp)(W1, b1, W2, b2)
        onehot = jax.nn.one_hot(expert_idx, e, dtype=x.dtype)
        next_states = jnp.einsum('te,etd->td', onehot, outs)
        out = p_max * next_states
        return out.reshape(b, s, d)
    x = L0_attn_x
    x = x + 0.5 * _L0_ffn_ref(_layernorm(x, axis=-1), L0_ffn_Wr, L0_ffn_W1, L0_ffn_b1, L0_ffn_W2, L0_ffn_b2)
    x = x + _L0_attn_ref(_layernorm(x, axis=-1), L0_attn_Wq, L0_attn_Wk, L0_attn_Wv, L0_attn_Wo)
    x = x + 0.5 * _L0_ffn_ref(_layernorm(x, axis=-1), L0_ffn_Wr, L0_ffn_W1, L0_ffn_b1, L0_ffn_W2, L0_ffn_b2)
    return x

_drawn_inputs = setup_inputs


def setup_inputs(seed=0):
    import zlib

    import numpy as np

    out = dict(_drawn_inputs(seed))
    spreads = {'L0_ffn_b1': (0.0, 0.292), 'L0_ffn_b2': (0.0, 0.1)}
    factors = {'L0_attn_Wq': 8.0, 'L0_attn_Wk': 8.0, 'L0_attn_Wv': 3.007, 'L0_attn_Wo': 3.046}
    for name, (base, spread) in spreads.items():
        noise = np.random.default_rng([zlib.crc32(name.encode()), seed]).standard_normal(out[name].shape)
        drawn = base * np.exp(spread * noise) if base else spread * noise
        out[name] = jnp.asarray(drawn.astype(out[name].dtype))
    for name, factor in factors.items():
        out[name] = (out[name] * factor).astype(out[name].dtype)
    return out
```

```python
from contextlib import ExitStack

import concourse.bass as bass
from concourse import mybir

P = 128
NB = 16
NT = 32
D = 128
H = 16
HD = 8
NE = 8
F = 512
FC = F // P
NS = NT + NE - 1
EPS = 1e-5
W1W = F + FC
VW = HD + 1
SPLIT = 6 * HD
KM = SPLIT + 6
KE = SPLIT + 9
QK_SCALE = float(HD) ** -0.25

ALU = mybir.AluOpType
ACT = mybir.ActivationFunctionType
AX = mybir.AxisListType
F32 = mybir.dt.float32
BF16 = mybir.dt.bfloat16
I32 = mybir.dt.int32


def build(nc, x, w1b, w2, b2, wr, wq, wk, wv, wo, cf, cb, qconst, kconst, out):
    ctx = ExitStack()
    with ctx:
        def sb(name, shape, dt=F32):
            return ctx.enter_context(nc.sbuf_tensor(name, shape, dt))

        def psum(name, shape, dt=F32):
            return ctx.enter_context(nc.psum_tensor(name, shape, dt))

        def sem(name):
            return ctx.enter_context(nc.semaphore(name))

        def dram(name, shape, dt=F32):
            return nc.dram_tensor(name, shape, dt, kind="Internal").ap()

        slot_x = dram("slot_x", [NS * P, D])
        slot_y = dram("slot_y", [NS * P, D])
        stack_q = [dram(f"stack_q{r}", [6, P, 256], BF16) for r in range(2)]
        stack_k = [dram(f"stack_k{r}", [6, P, 256], BF16) for r in range(2)]
        max_d = [dram(f"max_d{r}", [48, 256], BF16) for r in range(2)]

        x_sb = sb("x_sb", [P, NT, D])
        w2_sb = sb("w2_sb", [P, NE, FC, D])
        b2_sb = sb("b2_sb", [P, NE, D])
        wr_sb = sb("wr_sb", [P, NE])
        wqk_sb = sb("wqk_sb", [P, 2, D])
        wv_sb = sb("wv_sb", [P, D])
        wo_sb = sb("wo_sb", [P, D])
        cf_sb = sb("cf_sb", [P, cf.shape[1]])
        cb_sb = sb("cb_sb", [P, cb.shape[1]], BF16)
        ident_f = cf_sb[:, 0:P]
        steps128 = cf_sb[:, 128:160]
        keep = cf_sb[:, 160:416]
        rank8 = cf_sb[:, 416:424]
        slot_ids = cf_sb[:, 424:424 + NS]
        ones8 = cf_sb[:, 464:472]
        minus_half = cf_sb[:, 472:504]
        ident_b = cb_sb[:, 0:128]
        before = cb_sb[:, 128:256]
        ones_b = cb_sb[:, 256:384]
        mask_q = cb_sb[:, 384:512]
        mask_k = cb_sb[:, 512:640]

        xh_all = sb("xh_all", [P, NT, D])
        st_all = sb("st_all", [P, NT, 6])
        ln_a = sb("ln_a", [P, NT])
        ln_b = sb("ln_b", [P, NT])
        ln_c = sb("ln_c", [P, NT])
        mean_all = sb("mean_all", [P, NT])
        rstd_all = sb("rstd_all", [P, NT])
        xhT = [sb(f"xhT{r}", [P, 4 * P]) for r in range(2)]
        lmax = sb("lmax", [P, NT])
        lexp = sb("lexp", [P, NT, NE])
        cand = sb("cand", [P, NT, NE])
        chosen = sb("chosen", [P, NT])
        onehot = sb("onehot", [P, NE, NT], BF16)
        upto = sb("upto", [P, NE, NT])
        place = sb("place", [P, NE, NT])
        fills = sb("fills", [P, NE, NT])
        ntiles = sb("ntiles", [P, NE])
        tile_end = sb("tile_end", [P, NE])
        tile_start = sb("tile_start", [P, NE])
        expert_cmp = sb("expert_cmp", [P, NS, NE - 1])
        expert_f = sb("expert_f", [P, NS])
        expert_i = sb("expert_i", [P, NS], I32)
        slot_f = sb("slot_f", [P, NT])
        slot_i = sb("slot_i", [P, NT], I32)
        pmax = sb("pmax", [P, NT])
        zeros = sb("zeros", [P, 13, P])
        w1_st = [sb(f"w1_st{r}", [P, W1W]) for r in range(4)]
        xs = [sb(f"xs{r}", [P, D]) for r in range(4)]
        xsT = [sb(f"xsT{r}", [P, P]) for r in range(2)]
        hT = [sb(f"hT{r}", [P, FC, P]) for r in range(2)]
        ys = [sb(f"ys{r}", [P, D]) for r in range(4)]
        yg = [sb(f"yg{r}", [P, 2, D]) for r in range(2)]
        gidx = [sb(f"gidx{r}", [P, 2], I32) for r in range(2)]
        st2 = [sb(f"st2{r}", [P, 2, 6]) for r in range(2)]
        mv = [sb(f"mv{r}", [P, 2, 2]) for r in range(2)]
        veps = [sb(f"veps{r}", [P, 2]) for r in range(2)]
        rstd = [sb(f"rstd{r}", [P, 2]) for r in range(2)]
        xh = [sb(f"xh{r}", [P, 2, D]) for r in range(2)]
        xT = [sb(f"xT{r}", [P, 256]) for r in range(2)]
        rest = [sb(f"rest{r}", [P, 512]) for r in range(2)]
        parts = [sb(f"parts{r}", [P, 3, 2, 256], BF16) for r in range(2)]
        qs = [sb(f"qs{r}", [P, 8, 256], BF16) for r in range(2)]
        ks = [sb(f"ks{r}", [P, 8, 256], BF16) for r in range(2)]
        vaug = [sb(f"vaug{r}", [P, 2, H, VW]) for r in range(2)]
        nmax = [sb(f"nmax{r}", [P, 2, 2, 8]) for r in range(2)]
        nrest = sb("nrest", [P, 2, 2, 8])
        mparts = [sb(f"mparts{r}", [P, 2, 2, 3, 8], BF16) for r in range(2)]
        mT = [sb(f"mT{r}", [48, 256], BF16) for r in range(2)]
        pt0 = [sb(f"pt0{r}", [P, 4, 2, 2, 256]) for r in range(2)]
        pt1 = [sb(f"pt1{r}", [P, 2, 2, 4, 128]) for r in range(2)]
        rec = sb("rec", [P, 2 * H])
        o_sb = [sb(f"o_sb{r}", [P, 2 * H, HD]) for r in range(2)]
        oT = [sb(f"oT{r}", [P, 256]) for r in range(2)]

        pE = [psum(f"pE{r}", [P, 1024]) for r in range(2)]
        pM = [psum(f"pM{r}", [P, 512]) for r in range(2)]
        pA = psum("pA", [P, 512])
        pB = psum("pB", [P, 512])
        pO = pA[:, 0:2 * H * VW].rearrange("p (n w) -> p n w", w=VW)
        pMT = pB[0:48, 0:128].bitcast(BF16)

        names = """load_x load_w load_c zeroed slots_clear attn_vones
            res_stats ln_pow ln_xh xt_ps xt_sb qk_ps hi rest mid lo v_ps v_sb
            m_ps m_neg m_split mt_ps mt_sb e_ps e_sb pv_ps o_rec o_nrm ot_ps ot_sb wo_ps x_attn
            idx_sb res_x stats aggr veps mchain""".split()
        s = {n: sem(n) for n in names}
        load_xq = sem("load_xq")
        waited = sem("waited")
        got_y = [sem(f"got_y{r}") for r in range(2)]
        stack_w = [sem(f"stack_w{r}") for r in range(2)]
        stack_r = [sem(f"stack_r{r}") for r in range(2)]
        max_w = [sem(f"max_w{r}") for r in range(2)]
        max_r = [sem(f"max_r{r}") for r in range(2)]
        fs = []
        for f in range(2):
            g = {n: sem(f"{n}{f}") for n in """st lnst lnpow xh tr trc lg lexp lred route rank place
                scattered xT xTc up gelu down y ts""".split()}
            g["load"] = [sem(f"ld{f}_{r}") for r in range(4)]
            g["store"] = [sem(f"sto{f}_{r}") for r in range(4)]
            fs.append(g)
        fin_y = [sem(f"fin_y{r}") for r in range(2)]
        fin_o = [sem(f"fin_o{r}") for r in range(2)]
        fin_x = sem("fin_x")
        fin_idx = sem("fin_idx")

        block = ctx.enter_context(nc.Block())

        def at(B, per, more=0):
            m, c = B
            return per * c + more if isinstance(m, int) else m * (2 * per) + (per * c + more)

        def half(B, per, more=0):
            m, c = B
            return per * (c // 2) + more if isinstance(m, int) else m * per + (per * (c // 2) + more)

        def nxt(B, d):
            return (B[0], B[1] + d)

        def need(eng, semaphore, value):
            if isinstance(value, int) and value <= 0:
                return
            eng.wait_ge(semaphore, value)

        def alone(eng):
            eng.sem_inc(waited, 1)

        def steps(eng, step):
            step((0, 0))
            step((0, 1))
            with eng.Fori(1, 6) as m:
                step((m, 0))
                step((m, 1))
            for c in range(12, NB):
                step((0, c))

        def last(B):
            return B[1] if isinstance(B[0], int) else 11

        def first(B): return isinstance(B[0], int) and B[1] == 0
        def prj(B): return last(B) + 2 < NB
        def lnx(B): return last(B) + 3 < NB
        def mxx(B): return last(B) + 1 < NB
        def tiles(B):
            return bass.ds(at(B, 2), 2)

        @block.sync
        def _(sp):
            for q in range(4):
                sp.dma_start(x_sb[:, 8 * q:8 * q + 8, :],
                             x[8 * q * P:(8 * q + 8) * P, :].rearrange("(t p) d -> p t d", p=P)).then_inc(load_xq, 16)
            sp.dma_start(cf_sb[:], cf).then_inc(s["load_c"], 16)
            sp.dma_start(cb_sb[:], cb).then_inc(s["load_c"], 16)
            sp.dma_start(wr_sb[:], wr).then_inc(s["load_c"], 16)
            for q in range(3):
                if q == 0:
                    sp.wait_ge(s["zeroed"], 1)
                sp.dma_start(slot_x[q * 13 * P:(q + 1) * 13 * P, :].rearrange("(p t) d -> p t d", t=13),
                             zeros[:]).then_inc(s["slots_clear"], 16)
            sp.dma_start(w2_sb[:], w2.rearrange("e (c p) d -> p e c d", p=P)).then_inc(s["load_w"], 16)
            sp.dma_start(b2_sb[:], b2).then_inc(s["load_w"], 16)
            sp.dma_start(wqk_sb[:, 0, :], wq).then_inc(s["load_w"], 16)
            sp.dma_start(wqk_sb[:, 1, :], wk).then_inc(s["load_w"], 16)
            sp.dma_start(wv_sb[:], wv).then_inc(s["load_w"], 16)
            sp.dma_start(wo_sb[:], wo).then_inc(s["load_w"], 16)
            for r in range(2):
                for hh in range(2):
                    lo = hh * 64 + SPLIT
                    sp.dma_start(qs[r][lo:lo + 6, :, :], qconst[hh]).then_inc(s["load_w"], 16)
                    sp.dma_start(ks[r][lo:lo + 9, :, :], kconst[hh]).then_inc(s["load_w"], 16)

            def experts(f):
                g = fs[f]

                def load(m, c):
                    t = 4 * m + c if not isinstance(m, int) else c
                    r = c % 4
                    need(sp, g["up"], t - 3)
                    e = sp.value_load(expert_i[0:1, bass.ds(t, 1)], min_val=0, max_val=NE - 1)
                    sp.dma_start(w1_st[r][:], w1b[bass.ds(e, 1), :, :].rearrange("o p n -> p (o n)")).then_inc(g["load"][r], 16)
                    sp.dma_start(xs[r][:], slot_x[bass.ds(t * P, P), :]).then_inc(g["load"][r], 16)

                def store(m, c):
                    t = 4 * m + c if not isinstance(m, int) else c
                    sp.wait_ge(g["y"], t + 1)
                    alone(sp)
                    sp.dma_start(slot_y[bass.ds(t * P, P), :], ys[c % 4][:]).then_inc(g["store"][c % 4], 16)

                sp.wait_ge(g["ts"], 1)
                if f == 0:
                    sp.wait_ge(s["slots_clear"], 48)
                sp.wait_ge(g["scattered"], 16 * NT)
                for t in range(3):
                    load(0, t)
                load(0, 3)
                with sp.Fori(0, 8) as m:
                    for c in range(4):
                        store(m, c)
                        load(m, c + 4)
                for t in range(32, NS):
                    store(0, t)
                    if t + 4 < NS:
                        load(0, t + 4)

            experts(0)

            def stack_write(B):
                r = B[1] % 2
                need(sp, s["lo"], at(B, 1, 1))
                alone(sp)
                need(sp, stack_r[r], half(B, 64))
                for qk, dst, runs in ((0, stack_q[r], ((0, 3, 0, 0), (3, 2, 1, 0), (5, 1, 2, 0))),
                                      (1, stack_k[r], ((0, 3, 0, 1), (3, 2, 0, 1), (5, 1, 0, 1)))):
                    for c0, n, part, step in runs:
                        src = parts[r][:, part:part + (n if step else 1), qk, :]
                        if not step and n > 1:
                            src = src.to_broadcast([P, n, 256])
                        sp.dma_start(dst[c0:c0 + n, :, :].rearrange("c p t -> p c t"), src).then_inc(stack_w[r], 16)

            def stack_read(B):
                r = B[1] % 2
                sp.wait_ge(stack_w[r], half(B, 96, 96))
                alone(sp)
                need(sp, s["e_ps"], at(B, 6, -6))
                for dst, src in ((qs[r], stack_q[r]), (ks[r], stack_k[r])):
                    for hh in range(2):
                        sp.dma_start(dst[hh * 64:hh * 64 + SPLIT, :, :].rearrange("p g t -> p (g t)"),
                                     src[:, hh * 64:hh * 64 + 64, :].rearrange("c (d g) t -> c d (g t)", g=8)).then_inc(stack_r[r], 16)

            def max_rows(B):
                r = B[1] % 2
                sp.wait_ge(s["mt_sb"], at(B, 1, 1))
                alone(sp)
                need(sp, max_r[r], half(B, 32))
                sp.dma_start(max_d[r], mT[r][:]).then_inc(max_w[r], 16)
                sp.wait_ge(max_w[r], half(B, 16, 16))
                alone(sp)
                need(sp, s["e_ps"], at(B, 6, -6))
                for hh in range(2):
                    lo = hh * 64 + KM
                    sp.dma_start(qs[r][lo:lo + 3, :, :].rearrange("m g t -> m (g t)"),
                                 max_d[r][24 * hh:24 * hh + 24, :].rearrange("(m g) t -> m (g t)", g=8)).then_inc(max_r[r], 16)

            stack_write((0, 0))
            stack_read((0, 0))
            stack_write((0, 1))
            stack_read((0, 1))
            max_rows((0, 0))

            def sp_step(B):
                if prj(B):
                    stack_write(nxt(B, 2))
                    stack_read(nxt(B, 2))
                if mxx(B):
                    max_rows(nxt(B, 1))

            steps(sp, sp_step)
            experts(1)
            def store_out(m, c):
                sp.wait_ge(fin_x, 2 * m + c + 1)
                alone(sp)
                row = (m * 4 + 2 * c) * P
                sp.dma_start(out[bass.ds(row, 2 * P), :].rearrange("(t p) d -> p t d", p=P),
                             x_sb[:, bass.ds(m * 4 + 2 * c, 2), :]).then_inc(fin_o[c], 16)
            with sp.Fori(0, 8) as m:
                store_out(m, 0)
                store_out(m, 1)
            for r in range(2):
                sp.wait_ge(fin_o[r], 16 * 8)

        @block.gpsimd
        def _(pool):
            nc.gpsimd.memset(zeros[:], 0.0).then_inc(s["zeroed"], 1)

            def scatter(f):
                g = fs[f]
                pool.wait_ge(g["lnst"], 1)
                nc.gpsimd.tensor_tensor(rstd_all[:], ln_c[:], minus_half, ALU.pow).then_inc(g["lnpow"], 1)
                pool.wait_ge(g["place"], 1)
                if f == 0:
                    pool.wait_ge(s["slots_clear"], 48)
                for t in range(NT):
                    nc.gpsimd.indirect_dma_start(
                        out=slot_x, out_offset=bass.IndirectOffsetOnAxis(ap=slot_i[:, t:t + 1], axis=0),
                        in_=xh_all[:, t, :], in_offset=None).then_inc(g["scattered"], 16)

            def gather(B, sems, used, idx, base=0):
                r = B[1] % 2
                need(pool, sems[r], half(B, 32))
                nc.gpsimd.tensor_copy(gidx[r][:], slot_i[:, tiles(B)]).then_inc(idx, 1)
                pool.wait_ge(idx, at(B, 1, 1))
                need(pool, used, at(B, 1, -1))
                alone(pool)
                for j in range(2):
                    nc.gpsimd.indirect_dma_start(
                        out=yg[r][:, j, :], out_offset=None,
                        in_=slot_y, in_offset=bass.IndirectOffsetOnAxis(ap=gidx[r][:, j:j + 1], axis=0)).then_inc(sems[r], 16)

            scatter(0)
            for r in range(4):
                pool.wait_ge(fs[0]["store"][r], 16 * len(range(r, NS, 4)))

            def power(B):
                r = B[1] % 2
                pool.wait_ge(s["aggr"], at(B, 1, 1))
                alone(pool)
                nc.gpsimd.tensor_scalar(veps[r][:], mv[r][:, :, 1], EPS, None, ALU.add).then_inc(s["veps"], 1)
                pool.wait_ge(s["veps"], at(B, 1, 1))
                need(pool, s["ln_xh"], at(B, 1, -1))
                nc.gpsimd.tensor_tensor(rstd[r][:], veps[r][:], minus_half[:, 0:2], ALU.pow).then_inc(s["ln_pow"], 1)

            def low(B):
                r = B[1] % 2
                pool.wait_ge(s["mid"], at(B, 1, 1))
                nc.gpsimd.tensor_tensor(parts[r][:, 2, :, :], rest[r][:].rearrange("p (a t) -> p a t", a=2),
                                        parts[r][:, 1, :, :], ALU.subtract).then_inc(s["lo"], 1)

            g0 = lambda B: gather(B, got_y, s["res_x"], s["idx_sb"])
            g0((0, 0))
            g0((0, 1))
            power((0, 0))
            power((0, 1))
            g0((0, 2))
            low((0, 0))
            low((0, 1))
            power((0, 2))

            def pool_step(B):
                if lnx(B):
                    g0(nxt(B, 3))
                if prj(B):
                    low(nxt(B, 2))
                if lnx(B):
                    power(nxt(B, 3))

            steps(pool, pool_step)
            scatter(1)
            for r in range(4):
                pool.wait_ge(fs[1]["store"][r], 16 * len(range(r, NS, 4)))
            with pool.Fori(0, 8) as m:
                for c in range(2):
                    r = c
                    if c == 0:
                        pass
                    pool.wait_ge(fin_x, 2 * m + c + 0) if False else None
                    nc.gpsimd.tensor_copy(gidx[r][:], slot_i[:, bass.ds(m * 4 + 2 * c, 2)]).then_inc(fin_idx, 1)
                    pool.wait_ge(fin_idx, 2 * m + c + 1)
                    alone(pool)
                    for j in range(2):
                        nc.gpsimd.indirect_dma_start(
                            out=yg[r][:, j, :], out_offset=None,
                            in_=slot_y, in_offset=bass.IndirectOffsetOnAxis(ap=gidx[r][:, j:j + 1], axis=0)).then_inc(fin_y[r], 16)
                    pool.wait_ge(fin_x, 2 * m + c + 1)

        @block.scalar
        def _(act):
            def route(f):
                g = fs[f]
                with act.Fori(0, 4) as m:
                    for c in range(2):
                        act.wait_ge(g["tr"], 2 * m + c + 1)
                        if f == 0 and False:
                            pass
                        nc.scalar.activation(xhT[c][:], (pA, pB)[c][:], ACT.Copy).then_inc(g["trc"], 1)
                act.wait_ge(g["lred"], 2)
                nc.scalar.activation(lexp[:], cand[:], ACT.Exp).then_inc(g["lexp"], 1)

            def experts(f):
                g = fs[f]

                def gelu(m, c):
                    t = 4 * m + c if not isinstance(m, int) else c
                    act.wait_ge(g["up"], t + 1)
                    need(act, g["down"], t - 1)
                    for k in range(FC):
                        i = nc.scalar.activation(hT[c % 2][:, k, :], pE[0][:, (c % 2) * 512 + k * P:(c % 2) * 512 + (k + 1) * P],
                                                 ACT.Gelu, bias=w1_st[c % 4][:, F + k:F + k + 1])
                    i.then_inc(g["gelu"], 1)
                for c in range(2):
                    gelu(0, c)
                with act.Fori(0, 9) as m:
                    for c in range(2, 6):
                        gelu(m, c)
                gelu(0, 38)

            route(0)
            experts(0)

            def copy_x(B):
                act.wait_ge(s["xt_ps"], at(B, 1, 1))
                nc.scalar.activation(xT[B[1] % 2][:], pB[:, 0:256], ACT.Copy).then_inc(s["xt_sb"], 1)

            def high(B):
                r = B[1] % 2
                act.wait_ge(s["qk_ps"], at(B, 1, 1))
                need(act, stack_w[r], half(B, 96))
                nc.scalar.activation(parts[r][:, 0, :, :], pA[:].rearrange("p (a t) -> p a t", a=2), ACT.Copy,
                                     scale=QK_SCALE).then_inc(s["hi"], 1)

            def copy_m(B):
                act.wait_ge(s["mt_ps"], at(B, 1, 1))
                need(act, max_w[B[1] % 2], half(B, 16))
                nc.scalar.activation(mT[B[1] % 2][:], pMT, ACT.Copy).then_inc(s["mt_sb"], 1)

            def exps(B, u):
                r = B[1] % 2
                act.wait_ge(s["e_ps"], at(B, 6, u + 1))
                if u == 0:
                    need(act, s["pv_ps"], at(B, 1, -1))
                dst = pt0[r][:, u, :, :, :] if u < 4 else pt1[r][:, u - 4, :, :, :]
                w = 256 if u < 4 else 128
                nc.scalar.activation(dst, pE[u % 2][:].rearrange("p (a b t) -> p a b t", a=2, t=w), ACT.Exp).then_inc(s["e_sb"], 1)

            def copy_o(B):
                act.wait_ge(s["ot_ps"], at(B, 1, 1))
                nc.scalar.activation(oT[B[1] % 2][:], pB[:, 0:256], ACT.Copy).then_inc(s["ot_sb"], 1)

            for b in range(2):
                copy_x((0, b))
                high((0, b))
            copy_m((0, 0))

            def act_step(B):
                for u in range(6):
                    exps(B, u)
                    if u == 0 and prj(B):
                        copy_x(nxt(B, 2))
                    if u == 1 and prj(B):
                        high(nxt(B, 2))
                    if u == 2 and not first(B):
                        copy_o(nxt(B, -1))
                if mxx(B):
                    copy_m(nxt(B, 1))

            steps(act, act_step)
            copy_o((0, NB - 1))
            route(1)
            experts(1)

        @block.tensor
        def _(pe):
            pe.wait_ge(s["load_c"], 48)
            pe.wait_ge(s["load_w"], 16 * 14)

            def route(f):
                g = fs[f]
                if f == 1:
                    pe.wait_ge(s["x_attn"], NB)

                def turn(m, c):
                    pe.wait_ge(g["xh"], 2 * m + c + 1)
                    need(pe, g["trc"], 2 * m + c - 1)
                    for j in range(4):
                        i = pe.transpose((pA, pB)[c][:, j * P:(j + 1) * P], xh_all[:, m * 8 + c * 4 + j, :], ident_f)
                    i.then_inc(g["tr"], 1)

                def logits(m, c):
                    pe.wait_ge(g["trc"], 2 * m + c + 1)
                    for j in range(4):
                        i = pe.matmul(pM[0][:, m * 64 + c * 32 + j * 8:m * 64 + c * 32 + j * 8 + 8], xhT[c][:, j * P:(j + 1) * P], wr_sb[:],
                                      start=True, stop=True)
                    i.then_inc(g["lg"], 1)
                for m in range(4):
                    turn(m, 0)
                    turn(m, 1)
                    logits(m, 0)
                    logits(m, 1)
                pe.wait_ge(g["route"], 1)
                oh = onehot[:].rearrange("p e t -> p (e t)")
                pe.matmul(pM[1][:, 0:256], before, oh, start=True, stop=True)
                pe.matmul(pM[1][:, 256:512], ones_b, oh, start=True, stop=True).then_inc(g["rank"], 1)

            def experts(f):
                g = fs[f]

                def tile_no(m, c):
                    return 4 * m + c if not isinstance(m, int) else c

                def turn(m, c):
                    t = tile_no(m, c)
                    pe.wait_ge(g["load"][c % 4], 32 * m + 32 * (c // 4 + 1) if not isinstance(m, int) else 32 * (c // 4 + 1))
                    need(pe, g["xTc"], t - 1)
                    pe.transpose(pE[1][:, (c % 2) * 512:(c % 2) * 512 + P], xs[c % 4][:], ident_f).then_inc(g["xT"], 1)

                def up(m, c):
                    t = tile_no(m, c)
                    pe.wait_ge(g["xTc"], t + 1)
                    need(pe, g["gelu"], t - 1)
                    for k in range(FC):
                        i = pe.matmul(pE[0][:, (c % 2) * 512 + k * P:(c % 2) * 512 + (k + 1) * P],
                                      w1_st[c % 4][:, k * P:(k + 1) * P], xsT[c % 2][:], start=True, stop=True)
                    i.then_inc(g["up"], 1)

                def down(m, c):
                    t = tile_no(m, c)
                    e = pe.value_load(expert_i[0:1, bass.ds(t, 1)], min_val=0, max_val=NE - 1)
                    pe.wait_ge(g["gelu"], t + 1)
                    need(pe, g["y"], t - 1)
                    for k in range(FC):
                        i = pe.matmul(pM[c % 2][:, 0:D], hT[c % 2][:, k, :],
                                      w2_sb[:, bass.ds(e, 1), k, :].rearrange("p o d -> p (o d)"), start=(k == 0), stop=(k == FC - 1))
                    i.then_inc(g["down"], 1)

                pe.wait_ge(g["ts"], 1)
                turn(0, 0)
                turn(0, 1)
                up(0, 0)
                for c in range(1, 4):
                    turn(0, c + 1)
                    up(0, c)
                    down(0, c - 1)
                with pe.Fori(1, 9) as m:
                    for c in range(4):
                        turn(m, c + 1)
                        up(m, c)
                        down(m, c - 1)
                for c in range(36, 38):
                    turn(0, c + 1)
                    up(0, c)
                    down(0, c - 1)
                up(0, 38)
                down(0, 37)
                down(0, 38)

            route(0)
            experts(0)

            def turn_x(B):
                r = B[1] % 2
                pe.wait_ge(s["ln_xh"], at(B, 1, 1))
                need(pe, s["v_sb"], at(B, 1))
                need(pe, s["mt_sb"], at(B, 1, -1))
                for j in range(2):
                    i = pe.transpose(pB[:, j * P:(j + 1) * P], xh[r][:, j, :], ident_f)
                i.then_inc(s["xt_ps"], 1)

            def project_qk(B, free):
                r = B[1] % 2
                pe.wait_ge(s["xt_sb"], at(B, 1, 1))
                free()
                for a in range(2):
                    i = pe.matmul(pA[:, a * 256:(a + 1) * 256], wqk_sb[:, a, :], xT[r][:], start=True, stop=True)
                i.then_inc(s["qk_ps"], 1)

            def project_v(B):
                r = B[1] % 2
                for j in range(2):
                    i = pe.matmul(pB[:, 256 + j * P:256 + (j + 1) * P], xT[r][:, j * P:(j + 1) * P], wv_sb[:], start=True, stop=True)
                i.then_inc(s["v_ps"], 1)

            def m_unit(B, u):
                r, bank = B[1] % 2, pM[u % 2]
                if u == 0:
                    pe.wait_ge(stack_r[r], half(B, 64, 64))
                need(pe, s["m_ps"], at(B, 12, u)) if False else None
                need(pe, s["m_neg"], at(B, 12, u - 1))
                hh = u % 2
                if u < 8:
                    n, w, g0 = 2, 256, 2 * (u // 2)
                else:
                    n, w, g0 = 4, 128, 4 * ((u - 8) // 2)
                v = bank[:].rearrange("p (n w) -> p n w", w=w)
                q0 = 128 if u < 8 else 0
                pe.matmul(v[:, :, w - 128:w], ident_b, mask_q.rearrange("p (o k) -> p o k", o=1).to_broadcast([P, n, P]),
                          start=True, stop=False, skip_group_check=True)
                for j in range(n):
                    i = pe.matmul(v[:, j, :], qs[r][hh * 64:hh * 64 + KM, g0 + j, q0:q0 + 128],
                                  ks[r][hh * 64:hh * 64 + KM, g0 + j, 0:w], start=False, stop=(j == n - 1), skip_group_check=True)
                i.then_inc(s["m_ps"], 1)

            def e_unit(B, u):
                r = B[1] % 2
                if u == 0:
                    pe.wait_ge(max_r[r], half(B, 32, 32))
                need(pe, s["e_sb"], at(B, 6, u - 1))
                if u < 4:
                    n, w, g0, k0 = 2, 256, 2 * u, 0
                else:
                    n, w, g0, k0 = 4, 128, 4 * (u - 4), 128
                v = pE[u % 2][:].rearrange("p (a n w) -> p a n w", a=2, w=w)
                for hh in range(2):
                    pe.matmul(v[:, hh, :, 0:128], ident_b, mask_k.rearrange("p (o k) -> p o k", o=1).to_broadcast([P, n, P]),
                              start=True, stop=False, skip_group_check=True)
                for j in range(n):
                    for hh in range(2):
                        i = pe.matmul(v[:, hh, j, :], ks[r][hh * 64:hh * 64 + KE, g0 + j, k0:k0 + 128],
                                      qs[r][hh * 64:hh * 64 + KE, g0 + j, 256 - w:256], start=False, stop=(j == n - 1), skip_group_check=True)
                i.then_inc(s["e_ps"], 1)

            def attend(B, g):
                r = B[1] % 2
                for hh in range(2):
                    h = 2 * g + hh
                    a = pt0[r][:, g // 2, hh, g % 2, :]
                    b = pt1[r][:, g // 4, hh, g % 4, :]
                    pe.matmul(pO[:, h, :], a[:, 0:128], vaug[r][:, 0, h, :], start=True, stop=True)
                    pe.matmul(pO[:, H + h, :], a[:, 128:256], vaug[r][:, 0, h, :], start=True, stop=False)
                    i = pe.matmul(pO[:, H + h, :], b, vaug[r][:, 1, h, :], start=False, stop=True)
                return i

            def turn_m(B):
                r = B[1] % 2
                pe.wait_ge(s["m_split"], at(B, 1, 1))
                need(pe, s["x_attn"], at(B, 1, -1))
                alone(pe)
                for j in range(2):
                    i = pe.transpose(pMT[:, j * P:(j + 1) * P], mparts[r][:, j, :, :, :].rearrange("p a m g -> p (a m g)"), ident_b)
                i.then_inc(s["mt_ps"], 1)

            def turn_o(B):
                r = B[1] % 2
                pe.wait_ge(s["o_nrm"], at(B, 1, 1))
                v = o_sb[r][:].rearrange("p (a h) d -> p a (h d)", a=2)
                for j in range(2):
                    i = pe.transpose(pB[:, j * P:(j + 1) * P], v[:, j, :], ident_f)
                i.then_inc(s["ot_ps"], 1)

            def project_o(B):
                r = B[1] % 2
                pe.wait_ge(s["ot_sb"], at(B, 1, 1))
                for j in range(2):
                    i = pe.matmul(pB[:, 256 + j * P:256 + (j + 1) * P], oT[r][:, j * P:(j + 1) * P], wo_sb[:], start=True, stop=True)
                i.then_inc(s["wo_ps"], 1)

            for b in range(2):
                B = (0, b)
                turn_x(B)

                def free():
                    need(pe, s["hi"], b)
                    need(pe, s["rest"], b)
                project_qk(B, free)
                project_v(B)
            for u in range(12):
                m_unit((0, 0), u)
            pe.wait_ge(s["v_sb"], 2)
            turn_m((0, 0))

            def pe_step(B):
                for u in range(6):
                    e_unit(B, u)
                    if mxx(B):
                        m_unit(nxt(B, 1), 2 * u)
                        m_unit(nxt(B, 1), 2 * u + 1)
                    if u == 0 and prj(B):
                        turn_x(nxt(B, 2))
                    if u == 1 and prj(B):
                        project_qk(nxt(B, 2), lambda: need(pe, s["o_nrm"], at(B, 1)))
                    if u == 2 and not first(B):
                        if prj(B):
                            pe.wait_ge(s["xt_sb"], at(B, 1, 3))
                        else:
                            pe.wait_ge(s["mt_sb"], at(B, 1, 1))
                        turn_o(nxt(B, -1))
                    if u == 3 and not first(B):
                        project_o(nxt(B, -1))
                pe.wait_ge(s["e_sb"], at(B, 6, 6))
                pe.wait_ge(s["v_sb"], at(B, 1, 1))
                if prj(B):
                    pe.wait_ge(s["rest"], at(B, 1, 3))
                    pe.wait_ge(s["hi"], at(B, 1, 3))
                else:
                    need(pe, s["o_nrm"], at(B, 1))
                for g in range(4):
                    attend(B, g)
                if mxx(B):
                    turn_m(nxt(B, 1))
                for g in range(4, 8):
                    i = attend(B, g)
                i.then_inc(s["pv_ps"], 1)
                if prj(B):
                    pe.wait_ge(s["mt_sb"], at(B, 1, 2))
                    project_v(nxt(B, 2))

            steps(pe, pe_step)
            turn_o((0, NB - 1))
            project_o((0, NB - 1))
            route(1)
            experts(1)

        @block.vector
        def _(dve):
            V = nc.vector

            def route(f):
                g = fs[f]
                link = [0]

                def then(ins):
                    link[0] += 1
                    ins.then_inc(g["st"], 1)
                    dve.wait_ge(g["st"], link[0])

                with dve.Fori(0, 8) as m:
                    for j in range(4):
                        t = m * 4 + j
                        i = V.bn_stats(st_all[:, bass.ds(t, 1), :].rearrange("p o s -> p (o s)"), x_sb[:, bass.ds(t, 1), :].rearrange("p o d -> p (o d)"))
                    i.then_inc(g["st"], 1)
                link[0] = 8
                dve.wait_ge(g["st"], 8)
                me, mo, ve, vo = (st_all[:, :, k] for k in (1, 4, 2, 5))
                V.tensor_tensor(mean_all[:], me, mo, ALU.add)
                V.tensor_tensor(ln_a[:], me, mo, ALU.subtract)
                then(V.tensor_tensor(ln_b[:], ve, vo, ALU.add))
                then(V.scalar_tensor_tensor(ln_c[:], ln_a[:], 0.25, ln_a[:], ALU.mult, ALU.mult))
                then(V.scalar_tensor_tensor(ln_a[:], ln_b[:], 1.0 / D, ln_c[:], ALU.mult, ALU.add))
                V.tensor_scalar(ln_c[:], ln_a[:], EPS, None, ALU.add).then_inc(g["lnst"], 1)
                then(V.tensor_scalar(mean_all[:], mean_all[:], 0.5, None, ALU.mult))
                dve.wait_ge(g["lnpow"], 1)
                with dve.Fori(0, 8) as m:
                    for j in range(4):
                        t = m * 4 + j
                        i = V.tensor_scalar(xh_all[:, bass.ds(t, 1), :].rearrange("p o d -> p (o d)"), x_sb[:, bass.ds(t, 1), :].rearrange("p o d -> p (o d)"),
                                            mean_all[:, bass.ds(t, 1)], rstd_all[:, bass.ds(t, 1)],
                                            ALU.subtract, ALU.mult)
                    i.then_inc(g["xh"], 1)
                dve.wait_ge(g["lg"], 8)
                lg = pM[0][:, 0:NT * NE].rearrange("p (t e) -> p t e", e=NE)

                def per_tile(a):
                    return a.rearrange("p (t o) -> p t o", o=1).to_broadcast([P, NT, NE])
                then(V.tensor_reduce(lmax[:], lg, AX.X, ALU.max))
                V.tensor_tensor(cand[:], lg, per_tile(lmax[:]), ALU.subtract).then_inc(g["lred"], 2)
                dve.wait_ge(g["lexp"], 1)
                then(V.tensor_scalar(cand[:], cand[:], 0.0, None, ALU.is_equal))
                then(V.tensor_tensor(cand[:], cand[:], rank8.rearrange("p (o e) -> p o e", o=1).to_broadcast([P, NT, NE]), ALU.mult))
                then(V.tensor_reduce(chosen[:], cand[:], AX.X, ALU.max))
                V.tensor_tensor(onehot[:], rank8.rearrange("p (e o) -> p e o", o=1).to_broadcast([P, NE, NT]),
                                chosen[:].rearrange("p (o t) -> p o t", o=1).to_broadcast([P, NE, NT]), ALU.is_equal).then_inc(g["route"], 1)
                then(V.tensor_reduce(lmax[:], lexp[:], AX.X, ALU.add))
                then(V.reciprocal(pmax[:], lmax[:]))
                then(V.tensor_scalar(pmax[:], pmax[:], 0.5, None, ALU.mult))
                dve.wait_ge(g["rank"], 1)
                rank = pM[1][:, 0:256].rearrange("p (e t) -> p e t", e=NE)
                total = pM[1][:, 256:512].rearrange("p (e t) -> p e t", e=NE)
                then(V.tensor_copy(fills[:], total))
                then(V.tensor_tensor_scan(upto[:].rearrange("p e t -> p (e t)"), keep, fills[:].rearrange("p e t -> p (e t)"),
                                          0.0, ALU.mult, ALU.add))
                then(V.tensor_tensor(place[:], rank, upto[:], ALU.add))
                then(V.tensor_tensor(place[:], place[:], fills[:], ALU.subtract))
                then(V.tensor_tensor(fills[:], upto[:, :, NT - 1:NT].to_broadcast([P, NE, NT]),
                                     steps128.rearrange("p (o t) -> p o t", o=1).to_broadcast([P, NE, NT]), ALU.is_gt))
                then(V.tensor_reduce(ntiles[:], fills[:], AX.X, ALU.add))
                then(V.tensor_tensor_scan(tile_end[:], ones8, ntiles[:], 0.0, ALU.mult, ALU.add))
                then(V.tensor_tensor(tile_start[:], tile_end[:], ntiles[:], ALU.subtract))
                then(V.tensor_scalar(tile_start[:], tile_start[:], float(P), None, ALU.mult))
                then(V.tensor_tensor(place[:], place[:], tile_start[:].rearrange("p (e o) -> p e o", o=1).to_broadcast([P, NE, NT]), ALU.add))
                then(V.tensor_tensor(place[:], place[:], onehot[:], ALU.mult))
                then(V.tensor_reduce(slot_f[:], place[:].rearrange("p e t -> p t e"), AX.X, ALU.add))
                V.tensor_copy(slot_i[:], slot_f[:]).then_inc(g["place"], 1)
                then(V.tensor_tensor(expert_cmp[:], slot_ids.rearrange("p (s o) -> p s o", o=1).to_broadcast([P, NS, NE - 1]),
                                     tile_end[:, 0:NE - 1].rearrange("p (o e) -> p o e", o=1).to_broadcast([P, NS, NE - 1]), ALU.is_ge))
                then(V.tensor_reduce(expert_f[:], expert_cmp[:], AX.X, ALU.add))
                V.tensor_copy(expert_i[:], expert_f[:]).then_inc(g["ts"], 1)

            def experts(f):
                g = fs[f]

                def tile_no(m, c):
                    return 4 * m + c if not isinstance(m, int) else c

                def copy_x(m, c):
                    t = tile_no(m, c)
                    dve.wait_ge(g["xT"], t + 1)
                    need(dve, g["up"], t - 1)
                    V.tensor_copy(xsT[c % 2][:], pE[1][:, (c % 2) * 512:(c % 2) * 512 + P]).then_inc(g["xTc"], 1)

                def add_bias(m, c):
                    t = tile_no(m, c)
                    e = dve.value_load(expert_i[0:1, bass.ds(t, 1)], min_val=0, max_val=NE - 1)
                    if not isinstance(m, int) or c >= 4:
                        dve.wait_ge(g["store"][c % 4], 16 * m + 16 * (c // 4) if not isinstance(m, int) else 16 * (c // 4))
                    dve.wait_ge(g["down"], t + 1)
                    V.tensor_tensor(ys[c % 4][:], pM[c % 2][:, 0:D], b2_sb[:, bass.ds(e, 1), :].rearrange("p o d -> p (o d)"), ALU.add).then_inc(g["y"], 1)

                dve.wait_ge(g["ts"], 1)
                for c in range(5):
                    copy_x(0, c)
                    if c >= 1:
                        add_bias(0, c - 1)
                with dve.Fori(1, 9) as m:
                    for c in range(1, 5):
                        copy_x(m, c)
                        add_bias(m, c - 1)
                copy_x(0, 37)
                add_bias(0, 36)
                copy_x(0, 38)
                add_bias(0, 37)
                add_bias(0, 38)

            dve.wait_ge(load_xq, 64)
            dve.wait_ge(s["load_c"], 48)
            dve.wait_ge(s["load_w"], 16 * 14)
            for r in range(2):
                i = V.memset(vaug[r][:, :, :, HD], 1.0)
                i.then_inc(s["attn_vones"], 1)
            dve.wait_ge(s["attn_vones"], 2)
            route(0)
            experts(0)

            def residual(B):
                r = B[1] % 2
                dve.wait_ge(got_y[r], half(B, 32, 32))
                for j in range(2):
                    t = at(B, 2, j)
                    xt = x_sb[:, bass.ds(t, 1), :].rearrange("p o d -> p (o d)")
                    i = V.scalar_tensor_tensor(xt, yg[r][:, j, :], pmax[:, bass.ds(t, 1)], xt, ALU.mult, ALU.add)
                i.then_inc(s["res_x"], 1)
                dve.wait_ge(s["res_x"], at(B, 1, 1))
                alone(dve)
                for j in range(2):
                    t = at(B, 2, j)
                    i = V.bn_stats(st2[r][:, j, :], x_sb[:, bass.ds(t, 1), :].rearrange("p o d -> p (o d)"))
                i.then_inc(s["stats"], 1)
                dve.wait_ge(s["stats"], at(B, 1, 1))
                need(dve, s["veps"], at(B, 1, -1))
                alone(dve)
                for j in range(2):
                    i = V.bn_aggr(mv[r][:, j, :], st2[r][:, j, :])
                i.then_inc(s["aggr"], 1)

            def norm_x(B):
                r = B[1] % 2
                dve.wait_ge(s["ln_pow"], at(B, 1, 1))
                need(dve, s["xt_ps"], at(B, 1, -1))
                for j in range(2):
                    t = at(B, 2, j)
                    i = V.tensor_scalar(xh[r][:, j, :], x_sb[:, bass.ds(t, 1), :].rearrange("p o d -> p (o d)"), mv[r][:, j, 0:1],
                                        rstd[r][:, j:j + 1], ALU.subtract, ALU.mult)
                i.then_inc(s["ln_xh"], 1)

            def middle(B):
                r = B[1] % 2
                dve.wait_ge(s["hi"], at(B, 1, 1))
                need(dve, s["lo"], at(B, 1, -1))
                V.scalar_tensor_tensor(rest[r][:].rearrange("p (a t) -> p a t", a=2), pA[:].rearrange("p (a t) -> p a t", a=2),
                                       QK_SCALE, parts[r][:, 0, :, :], ALU.mult, ALU.subtract).then_inc(s["rest"], 1)
                dve.wait_ge(s["rest"], at(B, 1, 1))
                V.tensor_copy(parts[r][:, 1, :, :], rest[r][:].rearrange("p (a t) -> p a t", a=2)).then_inc(s["mid"], 1)

            def copy_v(B):
                r = B[1] % 2
                dve.wait_ge(s["v_ps"], at(B, 1, 1))
                need(dve, s["pv_ps"], at(B, 1, -1))
                V.tensor_copy(vaug[r][:, :, :, 0:HD], pB[:, 256:512].rearrange("p (a h d) -> p a h d", a=2, d=HD)).then_inc(s["v_sb"], 1)

            def m_reduce(B, u):
                r = B[1] % 2
                dve.wait_ge(s["m_ps"], at(B, 12, u + 1))
                if u == 0:
                    need(dve, s["mchain"], at(B, 3, -3))
                hh = u % 2
                if u < 8:
                    n, w, g0, blk = 2, 256, 2 * (u // 2), 1
                else:
                    n, w, g0, blk = 4, 128, 4 * ((u - 8) // 2), 0
                V.tensor_reduce(nmax[r][:, blk, hh, g0:g0 + n], pM[u % 2][:].rearrange("p (n w) -> p n w", w=w), AX.X, ALU.max,
                                negate=True).then_inc(s["m_neg"], 1)

            def m_split(B):
                r = B[1] % 2
                hi, mid, lo = (mparts[r][:, :, :, k, :].rearrange("p b a g -> p (b a) g") for k in range(3))
                nm = nmax[r][:].rearrange("p b a g -> p (b a) g")
                nr = nrest[:].rearrange("p b a g -> p (b a) g")
                dve.wait_ge(s["m_neg"], at(B, 12, 12))
                need(dve, s["mt_ps"], at(B, 1, -1))
                V.tensor_copy(hi, nm).then_inc(s["mchain"], 1)
                dve.wait_ge(s["mchain"], at(B, 3, 1))
                V.tensor_tensor(nr, nm, hi, ALU.subtract).then_inc(s["mchain"], 1)
                dve.wait_ge(s["mchain"], at(B, 3, 2))
                V.tensor_copy(mid, nr).then_inc(s["mchain"], 1)
                dve.wait_ge(s["mchain"], at(B, 3, 3))
                V.tensor_tensor(lo, nr, mid, ALU.subtract).then_inc(s["m_split"], 1)

            def norm_o(B):
                r = B[1] % 2
                dve.wait_ge(s["pv_ps"], at(B, 1, 1))
                need(dve, s["o_nrm"], at(B, 1))
                V.reciprocal(rec[:], pO[:, :, HD]).then_inc(s["o_rec"], 1)
                dve.wait_ge(s["o_rec"], at(B, 1, 1))
                need(dve, s["ot_ps"], at(B, 1, -1))
                V.tensor_tensor(o_sb[r][:], pO[:, :, 0:HD], rec[:].rearrange("p (n o) -> p n o", o=1).to_broadcast([P, 2 * H, HD]),
                                ALU.mult).then_inc(s["o_nrm"], 1)

            def add_attn(B):
                dve.wait_ge(s["wo_ps"], at(B, 1, 1))
                xt = x_sb[:, tiles(B), :].rearrange("p a d -> p (a d)")
                V.tensor_tensor(xt, pB[:, 256:512], xt, ALU.add).then_inc(s["x_attn"], 1)

            residual((0, 0))
            residual((0, 1))
            norm_x((0, 0))
            norm_x((0, 1))
            middle((0, 0))
            copy_v((0, 0))
            middle((0, 1))
            copy_v((0, 1))
            residual((0, 2))
            norm_x((0, 2))
            for u in range(12):
                m_reduce((0, 0), u)
            m_split((0, 0))

            def dve_step(B):
                for u in range(12):
                    if mxx(B):
                        m_reduce(nxt(B, 1), u)
                    if u == 3 and prj(B):
                        middle(nxt(B, 2))
                    if u == 4 and lnx(B):
                        residual(nxt(B, 3))
                    if u == 8 and lnx(B):
                        norm_x(nxt(B, 3))
                    if u == 9 and not first(B):
                        add_attn(nxt(B, -1))
                if mxx(B):
                    m_split(nxt(B, 1))
                norm_o(B)
                if prj(B):
                    copy_v(nxt(B, 2))

            steps(dve, dve_step)
            add_attn((0, NB - 1))
            dve.wait_ge(s["x_attn"], NB)
            route(1)
            experts(1)
            with dve.Fori(0, 8) as m:
                for c in range(2):
                    dve.wait_ge(fin_y[c], 32 * m + 32)
                    for j in range(2):
                        t = m * 4 + 2 * c + j
                        xt = x_sb[:, bass.ds(t, 1), :].rearrange("p o d -> p (o d)")
                        i = V.scalar_tensor_tensor(xt, yg[c][:, j, :], pmax[:, bass.ds(t, 1)], xt, ALU.mult, ALU.add)
                    i.then_inc(fin_x, 1)


def kernel(L0_attn_x, L0_attn_Wq, L0_attn_Wk, L0_attn_Wv, L0_attn_Wo, L0_ffn_Wr, L0_ffn_W1, L0_ffn_b1, L0_ffn_W2, L0_ffn_b2):
    import numpy as np
    import concourse.bacc as bacc
    from concourse.bass_utils import run_bass_kernel_spmd

    f32 = np.float32
    bf16 = mybir.dt.np(BF16) if hasattr(mybir.dt, "np") else __import__("ml_dtypes").bfloat16
    c = np.ascontiguousarray

    w1b = np.concatenate([L0_ffn_W1, L0_ffn_b1.reshape(NE, FC, P).transpose(0, 2, 1)], axis=2)
    order = np.array([(2 * g + hh) * HD + d for hh in range(2) for d in range(HD) for g in range(8)])

    cf = np.zeros((P, 512), f32)
    cf[:, 0:128] = np.eye(P)
    cf[:, 128:160] = np.arange(32) * 128
    cf[:, 160:416] = (np.arange(256) % 32 != 0)
    cf[:, 416:424] = 8 - np.arange(8)
    cf[:, 424:424 + NS] = np.arange(NS)
    cf[:, 464:472] = 1
    cf[:, 472:504] = -0.5
    i = np.arange(P)
    cb = np.zeros((P, 640), f32)
    cb[:, 0:128] = np.eye(P)
    cb[:, 128:256] = i[:, None] < i[None, :]
    cb[:, 256:384] = 1
    cb[:, 384:512] = np.where(i[None, :] > i[:, None], -1e30, 0)
    cb[:, 512:640] = np.where(i[:, None] > i[None, :], -1e30, 0)

    def three(a):
        hi = a.astype(bf16)
        mid = (a - hi.astype(np.float64)).astype(bf16)
        lo = (a - hi.astype(np.float64) - mid.astype(np.float64)).astype(bf16)
        return hi, mid, lo

    base = 2.0 ** (-8.0 / H)
    slopes = np.array([base ** n for n in range(1, H + 1)], dtype=f32).astype(np.float64)
    qconst = np.ones((2, 6, 8, 256), bf16)
    kconst = np.ones((2, 9, 8, 256), bf16)
    for hh in range(2):
        for g in range(8):
            bias = three(slopes[2 * g + hh] * (np.arange(256) - 128.0))
            for n in range(3):
                kconst[hh, n, g] = bias[n]
                qconst[hh, 3 + n, g] = -bias[n]

    arrays = {
        "x": c(L0_attn_x.reshape(NT * P, D)), "w1b": c(w1b), "w2": c(L0_ffn_W2),
        "b2": c(np.broadcast_to(L0_ffn_b2.reshape(1, NE * D), (P, NE * D))), "wr": c(L0_ffn_Wr),
        "wq": c(L0_attn_Wq[order].T), "wk": c(L0_attn_Wk[order].T), "wv": c(L0_attn_Wv.T), "wo": c(L0_attn_Wo.T),
        "cf": cf, "cb": cb.astype(bf16), "qconst": qconst, "kconst": kconst,
    }
    nc = bacc.Bacc("TRN2", target_bir_lowering=False, num_devices=1)
    args = []
    for name, a in arrays.items():
        args.append(nc.dram_tensor(f"in_{name}", a.shape, mybir.dt.from_np(a.dtype), kind="ExternalInput").ap())
    out = nc.dram_tensor("out", (NT * P, D), F32, kind="ExternalOutput").ap()
    build(nc, *args, out)
    r = run_bass_kernel_spmd(nc, [{f"in_{n}": a for n, a in arrays.items()}], core_ids=[0])
    return r.results[0]["out"].reshape(NB, 256, D)
```

```python
from contextlib import ExitStack

import concourse.bass as bass
from concourse import mybir

P = 128
NB = 16
NT = 32
D = 128
H = 16
HD = 8
NE = 8
F = 512
FC = F // P
TG = NT // 2
NSG = TG + NE - 1
NS = 2 * NSG
EPS = 1e-5
W1W = F + FC + D
VW = 32
SPLIT = 6 * HD
KM = SPLIT + 6
KE = SPLIT + 9
PT0 = H * 256
PT1 = H * 128
QK_SCALE = float(HD) ** -0.25

ALU = mybir.AluOpType
ACT = mybir.ActivationFunctionType
AX = mybir.AxisListType
F32 = mybir.dt.float32
BF16 = mybir.dt.bfloat16
I32 = mybir.dt.int32


def build(nc, x, w1b, w2, wr, wq, wk, wv, wo, cf, cb, qconst, kconst, out):
    ctx = ExitStack()
    with ctx:
        def sb(name, shape, dt=F32):
            return ctx.enter_context(nc.sbuf_tensor(name, shape, dt))

        def psum(name, shape, dt=F32):
            return ctx.enter_context(nc.psum_tensor(name, shape, dt))

        def sem(name):
            return ctx.enter_context(nc.semaphore(name))

        def dram(name, shape, dt=F32):
            return nc.dram_tensor(name, shape, dt, kind="Internal").ap()

        slot_x = [dram(f"slot_x{g}", [NSG * P, D]) for g in range(2)]
        slot_y = [dram(f"slot_y{g}", [NSG * P, D]) for g in range(2)]
        stack_q = [dram(f"stack_q{r}", [6, P, 256], BF16) for r in range(2)]
        stack_k = [dram(f"stack_k{r}", [6, P, 256], BF16) for r in range(2)]
        max_d = [dram(f"max_d{r}", [48, 256], BF16) for r in range(2)]

        x_sb = sb("x_sb", [P, NT, D])
        w1_sb = sb("w1_sb", [P, NE, W1W])
        w2_sb = sb("w2_sb", [P, NE, FC, D])
        wr_sb = sb("wr_sb", [P, NE])
        wqk_sb = sb("wqk_sb", [P, 2, D])
        wv_sb = sb("wv_sb", [P, D])
        wo_sb = sb("wo_sb", [P, D])
        cf_sb = sb("cf_sb", [P, cf.shape[1]])
        cb_sb = sb("cb_sb", [P, cb.shape[1]], BF16)
        ident_f = cf_sb[:, 0:P]
        steps128 = cf_sb[:, 128:128 + TG]
        keep = cf_sb[:, 160:160 + NE * TG]
        rank8 = cf_sb[:, 416:424]
        slot_ids = cf_sb[:, 424:424 + NSG]
        ones8 = cf_sb[:, 464:472]
        minus_half = cf_sb[:, 472:504]
        ident_b = cb_sb[:, 0:128]
        before = cb_sb[:, 128:256]
        ones_b = cb_sb[:, 256:384]
        mask_q = cb_sb[:, 384:512]
        mask_k = cb_sb[:, 512:640]

        xh_all = sb("xh_all", [P, NT, D])
        st_all = sb("st_all", [P, NT, 6])
        ln_a = sb("ln_a", [P, TG])
        ln_b = sb("ln_b", [P, TG])
        ln_c = sb("ln_c", [P, NT])
        mean_all = sb("mean_all", [P, NT])
        rstd_all = sb("rstd_all", [P, NT])
        lg_all = sb("lg_all", [P, NT, NE])
        lmax = sb("lmax", [P, TG])
        lexp = sb("lexp", [P, TG, NE])
        cand = sb("cand", [P, TG, NE])
        equal = sb("equal", [P, TG, NE])
        chosen = sb("chosen", [P, TG])
        onehot = sb("onehot", [P, NE, TG], BF16)
        upto = sb("upto", [P, NE, TG])
        place = sb("place", [P, NE, TG])
        fills = sb("fills", [P, NE, TG])
        ntiles = sb("ntiles", [P, NE])
        tile_end = sb("tile_end", [P, NE])
        tile_start = sb("tile_start", [P, NE])
        expert_cmp = sb("expert_cmp", [P, NSG, NE - 1])
        expert_f = sb("expert_f", [P, NSG])
        expert_i = sb("expert_i", [P, NS], I32)
        slot_f = sb("slot_f", [P, TG])
        slot_i = sb("slot_i", [P, NT], I32)
        pmax = sb("pmax", [P, NT])
        st3 = [sb(f"st3{r}", [P, 2, 6]) for r in range(2)]
        mv3 = [sb(f"mv3{r}", [P, 2, 2]) for r in range(2)]
        veps3 = [sb(f"veps3{r}", [P, 2]) for r in range(2)]
        rstd3 = [sb(f"rstd3{r}", [P, 2]) for r in range(2)]
        xr = [sb(f"xr{r}", [P, 2, D]) for r in range(2)]
        xrT = sb("xrT", [P, 256])
        region = [sb(f"region{r}", [P, PT0 + PT1]) for r in range(2)]
        pt0 = [a[:, 0:PT0].rearrange("p (u a b t) -> p u a b t", u=4, a=2, b=2) for a in region]
        pt1 = [a[:, PT0:].rearrange("p (u a b t) -> p u a b t", u=2, a=2, b=4) for a in region]
        zeros = region[1][:, 0:NSG * P].rearrange("p (a b) -> p a b", b=P)
        xhT = [region[0][:, 4096 + r * 512:4608 + r * 512] for r in range(2)]
        w1_st = [region[0][:, r * W1W:(r + 1) * W1W] for r in range(4)]
        xs = [region[0][:, 4 * W1W + r * D:4 * W1W + (r + 1) * D] for r in range(4)]
        hT = [region[1][:, 3072 + r * F:3072 + (r + 1) * F].rearrange("p (k t) -> p k t", k=FC) for r in range(2)]
        xsT = [region[1][:, 4096 + r * P:4096 + (r + 1) * P] for r in range(2)]
        ys = [region[1][:, 4352 + r * D:4352 + (r + 1) * D] for r in range(4)]
        st2 = [sb(f"st2{r}", [P, 2, 6]) for r in range(2)]
        mv = [sb(f"mv{r}", [P, 2, 2]) for r in range(2)]
        veps = [sb(f"veps{r}", [P, 2]) for r in range(2)]
        rstd = [sb(f"rstd{r}", [P, 2]) for r in range(2)]
        xh = [sb(f"xh{r}", [P, 2, D]) for r in range(2)]
        xT = [sb(f"xT{r}", [P, 256]) for r in range(4)]
        rest = sb("rest", [P, 512])
        parts = [sb(f"parts{r}", [P, 3, 2, 256], BF16) for r in range(2)]
        qs = [sb(f"qs{r}", [P, 8, 256], BF16) for r in range(4)]
        ks = [sb(f"ks{r}", [P, 8, 256], BF16) for r in range(4)]
        vaug = [sb(f"vaug{r}", [P, 2, H, VW]) for r in range(2)]
        nmax = [sb(f"nmax{r}", [P, 2, 2, 8]) for r in range(2)]
        nrest = sb("nrest", [P, 2, 2, 8])
        mparts = [sb(f"mparts{r}", [P, 2, 2, 3, 8], BF16) for r in range(2)]
        mT = [sb(f"mT{r}", [48, 256], BF16) for r in range(2)]
        outT = [sb(f"outT{r}", [P, 512]) for r in range(2)]
        rec = sb("rec", [P, 2, 8])
        o_sb = [sb(f"o_sb{r}", [P, 2, D]) for r in range(2)]
        oT = [sb(f"oT{r}", [P, 256]) for r in range(2)]

        pE = psum("pE", [P, 1024])
        pM = [psum(f"pM{r}", [P, 512]) for r in range(2)]
        pA = psum("pA", [P, 512])
        pB = psum("pB", [P, 512])
        pO = psum("pO", [P, 512])
        pC = psum("pC", [P, 512])
        pMT = pB[0:48, 0:128].bitcast(BF16)

        names = """load_w load_c zeroed slots_clear attn_vones
            hi rest mid lo v_ps v_sb xt_ps xt_sb qk_ps ln_pow ln_xh
            m_ps m_neg m_split mt_ps mt_sb e_ps e_sb pv_ps pv_sb back_ps o_rec o_nrm ot_ps ot_sb wo_ps x_attn
            res_x stats aggr veps mchain
            r_stats r_aggr r_veps r_pow r_xh r_copied r_tps r_tsb r_lps r_lg
            st lnst lnpow xh tr trc lg chain diff lexp route rank ranks_sb place ts fin_x fin_x0""".split()
        s = {n: sem(n) for n in names}
        waited = sem("waited")
        load_x = [sem(f"load_x{q}") for q in range(4)]
        got_y = [sem(f"got_y{g}") for g in range(2)]
        stack_w = [sem(f"stack_w{r}") for r in range(2)]
        stack_r = [sem(f"stack_r{r}") for r in range(4)]
        max_w = [sem(f"max_w{r}") for r in range(2)]
        max_r = [sem(f"max_r{r}") for r in range(4)]
        fs = []
        for f in range(2):
            e = {n: sem(f"{n}{f}") for n in "w1c xT xTc up gelu down y".split()}
            e["scattered"] = [sem(f"scattered{f}_{g}") for g in range(2)]
            e["load"] = [sem(f"ld{f}_{r}") for r in range(4)]
            e["store"] = [sem(f"sto{f}_{r}") for r in range(4)]
            fs.append(e)
        fin_y = [sem(f"fin_y{k}") for k in range(5)]
        fin_o = sem("fin_o")

        LOADED = 16 * (6 + 4 * 2 * 2)

        block = ctx.enter_context(nc.Block())

        def at(B, per, more=0):
            m, c = B
            return per * c + more if isinstance(m, int) else m * (4 * per) + (per * c + more)

        def half(B, per, more=0):
            m, c = B
            return per * (c // 2) + more if isinstance(m, int) else m * (2 * per) + (per * (c // 2) + more)

        def quarter(B, per, more=0):
            m, c = B
            return per * (c // 4) + more if isinstance(m, int) else m * per + (per * (c // 4) + more)

        def nxt(B, d):
            return (B[0], B[1] + d)

        def need(eng, semaphore, value):
            if isinstance(value, int) and value <= 0:
                return
            eng.wait_ge(semaphore, value)

        def alone(eng):
            eng.sem_inc(waited, 1)

        def steps(eng, step):
            for c in range(4):
                step((0, c))
            with eng.Fori(1, 3) as m:
                for c in range(4):
                    step((m, c))
            for c in range(12, NB + 3):
                step((0, c))

        def is_step(B, c):
            return isinstance(B[0], int) and B[1] == c

        def has(B, d):
            return not isinstance(B[0], int) or 0 <= B[1] + d < NB

        def tiles(B):
            return bass.ds(at(B, 2), 2)

        @block.sync
        def _(sp):
            sp.dma_start(x_sb[:, 0:8, :], x[0:8 * P, :].rearrange("(t p) d -> p t d", p=P)).then_inc(load_x[0], 16)
            sp.dma_start(cf_sb[:], cf).then_inc(s["load_c"], 16)
            sp.dma_start(wr_sb[:], wr).then_inc(s["load_c"], 16)
            sp.dma_start(cb_sb[:], cb).then_inc(s["load_c"], 16)
            for q in range(1, 4):
                sp.dma_start(x_sb[:, 8 * q:8 * q + 8, :],
                             x[8 * q * P:(8 * q + 8) * P, :].rearrange("(t p) d -> p t d", p=P)).then_inc(load_x[q], 16)
            sp.wait_ge(s["zeroed"], 1)
            for g in range(2):
                sp.dma_start(slot_x[g].rearrange("(p t) d -> p t d", t=NSG),
                             zeros).then_inc(s["slots_clear"], 16)
            sp.dma_start(w1_sb[:], w1b.rearrange("e p n -> p e n")).then_inc(s["load_w"], 16)
            sp.dma_start(w2_sb[:], w2.rearrange("e (c p) d -> p e c d", p=P)).then_inc(s["load_w"], 16)
            sp.dma_start(wqk_sb[:, 0, :], wq).then_inc(s["load_w"], 16)
            sp.dma_start(wqk_sb[:, 1, :], wk).then_inc(s["load_w"], 16)
            sp.dma_start(wv_sb[:], wv).then_inc(s["load_w"], 16)
            sp.dma_start(wo_sb[:], wo).then_inc(s["load_w"], 16)
            for r in range(4):
                for hh in range(2):
                    lo = hh * 64 + SPLIT
                    sp.dma_start(qs[r][lo:lo + 6, :, :], qconst[hh]).then_inc(s["load_w"], 16)
                    sp.dma_start(ks[r][lo:lo + 9, :, :], kconst[hh]).then_inc(s["load_w"], 16)

            def experts(f):
                e = fs[f]

                def ready(g):
                    if g == 0 and f == 1:
                        sp.wait_ge(s["pv_ps"], 2 * NB)
                    sp.wait_ge(e["scattered"][g], 16 * TG)

                def load(g, m, c):
                    t = 4 * m + c
                    need(sp, e["xT"], t - 3)
                    if not isinstance(m, int):
                        alone(sp)
                    sp.dma_start(xs[c % 4], slot_x[g][bass.ds((t - NSG * g) * P, P), :]).then_inc(e["load"][c % 4], 16)

                def store(g, m, c):
                    t = 4 * m + c
                    sp.wait_ge(e["y"], t + 1)
                    alone(sp)
                    sp.dma_start(slot_y[g][bass.ds((t - NSG * g) * P, P), :], ys[c % 4]).then_inc(e["store"][c % 4], 16)

                ready(0)
                for t in range(6):
                    load(0, 0, t)
                    if t >= 4:
                        store(0, 0, t - 4)
                with sp.Fori(1, 5) as m:
                    for c in range(2, 6):
                        load(0, m, c)
                        store(0, m, c - 4)
                for t in range(22, 27):
                    if t == NSG:
                        ready(1)
                    load(t // NSG, 0, t)
                    store(0, 0, t - 4)
                with sp.Fori(6, 10) as m:
                    for c in range(3, 7):
                        load(1, m, c)
                        store(1, m, c - 4)
                for t in range(43, NS):
                    load(1, 0, t)
                    store(1, 0, t - 4)
                for t in range(NS - 4, NS):
                    store(1, 0, t)

            experts(0)

            def stack_write(B):
                r = B[1] % 2
                need(sp, s["lo"], at(B, 1, 1))
                alone(sp)
                if has(B, -2):
                    sp.wait_ge(stack_r[(B[1] - 2) % 4], quarter(nxt(B, -2), 64, 64))
                    alone(sp)
                for qk, dst, runs in ((0, stack_q[r], ((0, 3, 0, 0), (3, 2, 1, 0), (5, 1, 2, 0))),
                                      (1, stack_k[r], ((0, 3, 0, 1), (3, 2, 0, 1), (5, 1, 0, 1)))):
                    for c0, n, part, step in runs:
                        src = parts[r][:, part:part + (n if step else 1), qk, :]
                        if not step and n > 1:
                            src = src.to_broadcast([P, n, 256])
                        sp.dma_start(dst[c0:c0 + n, :, :].rearrange("c p t -> p c t"), src).then_inc(stack_w[r], 16)

            def stack_read(B):
                r, r4 = B[1] % 2, B[1] % 4
                sp.wait_ge(stack_w[r], half(B, 96, 96))
                alone(sp)
                need(sp, s["e_ps"], at(B, 6, -18))
                alone(sp)
                for dst, src in ((qs[r4], stack_q[r]), (ks[r4], stack_k[r])):
                    for hh in range(2):
                        sp.dma_start(dst[hh * 64:hh * 64 + SPLIT, :, :].rearrange("p g t -> p (g t)"),
                                     src[:, hh * 64:hh * 64 + 64, :].rearrange("c (d g) t -> c d (g t)", g=8)).then_inc(stack_r[r4], 16)

            def max_rows(B):
                r, r4 = B[1] % 2, B[1] % 4
                sp.wait_ge(s["mt_sb"], at(B, 1, 1))
                alone(sp)
                if has(B, -2):
                    sp.wait_ge(max_r[(B[1] - 2) % 4], quarter(nxt(B, -2), 32, 32))
                    alone(sp)
                sp.dma_start(max_d[r], mT[r][:]).then_inc(max_w[r], 16)
                sp.wait_ge(max_w[r], half(B, 16, 16))
                alone(sp)
                need(sp, s["e_ps"], at(B, 6, -18))
                alone(sp)
                for hh in range(2):
                    lo = hh * 64 + KM
                    sp.dma_start(qs[r4][lo:lo + 3, :, :].rearrange("m g t -> m (g t)"),
                                 max_d[r][24 * hh:24 * hh + 24, :].rearrange("(m g) t -> m (g t)", g=8)).then_inc(max_r[r4], 16)

            for b in range(2):
                stack_write((0, b))
                stack_read((0, b))
            max_rows((0, 0))

            def sp_step(B):
                if has(B, 2):
                    stack_write(nxt(B, 2))
                    stack_read(nxt(B, 2))
                if has(B, 1):
                    max_rows(nxt(B, 1))

            steps(sp, sp_step)
            experts(1)
            def store_out(t, n):
                sp.dma_start(out[t * P:(t + n) * P, :].rearrange("(t p) d -> p t d", p=P), x_sb[:, t:t + n, :]).then_inc(fin_o, 16)

            sp.wait_ge(s["fin_x0"], 2)
            store_out(0, 8)
            store_out(8, 8)
            for k in range(4):
                sp.wait_ge(s["fin_x"], k + 1)
                store_out(TG + 4 * k, 4)
            sp.wait_ge(fin_o, 16 * 6)

        @block.gpsimd
        def _(pool):
            nc.gpsimd.memset(zeros, 0.0).then_inc(s["zeroed"], 1)

            def scatter(f, g):
                n = 2 * f + g
                pool.wait_ge(s["place"], n + 1)
                if n == 0:
                    pool.wait_ge(s["slots_clear"], 32)
                if f == 1:
                    pool.wait_ge(s["r_copied"], 8 * (g + 1))
                for t in range(TG * g, TG * g + TG):
                    nc.gpsimd.indirect_dma_start(
                        out=slot_x[g], out_offset=bass.IndirectOffsetOnAxis(ap=slot_i[:, t:t + 1], axis=0),
                        in_=xh_all[:, t, :], in_offset=None).then_inc(fs[f]["scattered"][g], 16)

            def stored(f, g):
                for r in range(4):
                    pool.wait_ge(fs[f]["store"][r], 16 * len(range(r, NSG * (g + 1), 4)))

            def gather(t, semaphore):
                nc.gpsimd.indirect_dma_start(
                    out=xh_all[:, t, :], out_offset=None,
                    in_=slot_y[t // TG], in_offset=bass.IndirectOffsetOnAxis(ap=slot_i[:, t:t + 1], axis=0)).then_inc(semaphore, 16)

            for g in range(2):
                pool.wait_ge(s["lnst"], g + 1)
                nc.gpsimd.tensor_tensor(rstd_all[:, TG * g:TG * g + TG], ln_c[:, TG * g:TG * g + TG], minus_half[:, 0:TG],
                                        ALU.pow).then_inc(s["lnpow"], 1)
            scatter(0, 0)
            scatter(0, 1)
            stored(0, 0)
            for t in range(TG):
                gather(t, got_y[0])

            def power(B):
                r = B[1] % 2
                pool.wait_ge(s["aggr"], at(B, 1, 1))
                alone(pool)
                nc.gpsimd.tensor_scalar(veps[r][:], mv[r][:, :, 1], EPS, None, ALU.add).then_inc(s["veps"], 1)
                pool.wait_ge(s["veps"], at(B, 1, 1))
                need(pool, s["ln_xh"], at(B, 1, -1))
                nc.gpsimd.tensor_tensor(rstd[r][:], veps[r][:], minus_half[:, 0:2], ALU.pow).then_inc(s["ln_pow"], 1)

            def low(B):
                r = B[1] % 2
                pool.wait_ge(s["mid"], at(B, 1, 1))
                nc.gpsimd.tensor_tensor(parts[r][:, 2, :, :], rest[:].rearrange("p (a t) -> p a t", a=2),
                                        parts[r][:, 1, :, :], ALU.subtract).then_inc(s["lo"], 1)

            def r_power(B):
                r = B[1] % 2
                pool.wait_ge(s["r_aggr"], at(B, 1, 1))
                alone(pool)
                nc.gpsimd.tensor_scalar(veps3[r][:], mv3[r][:, :, 1], EPS, None, ALU.add).then_inc(s["r_veps"], 1)
                pool.wait_ge(s["r_veps"], at(B, 1, 1))
                need(pool, s["r_xh"], at(B, 1, -1))
                nc.gpsimd.tensor_tensor(rstd3[r][:], veps3[r][:], minus_half[:, 0:2], ALU.pow).then_inc(s["r_pow"], 1)

            power((0, 0))
            power((0, 1))
            low((0, 0))
            low((0, 1))
            power((0, 2))

            def pool_step(B):
                if is_step(B, 0):
                    stored(0, 1)
                if isinstance(B[0], int) and B[1] < 4:
                    for t in range(4):
                        gather(TG + 4 * B[1] + t, got_y[1])
                if has(B, 2):
                    low(nxt(B, 2))
                if has(B, 3):
                    power(nxt(B, 3))
                if has(B, -2):
                    r_power(nxt(B, -2))
                if is_step(B, 13):
                    scatter(1, 0)

            steps(pool, pool_step)
            scatter(1, 1)
            stored(1, 0)
            for t in range(TG):
                gather(t, fin_y[4])
            pool.wait_ge(fin_y[4], 16 * TG)
            nc.gpsimd.tensor_tensor(xh_all[:, 0:TG, :], xh_all[:, 0:TG, :],
                                    pmax[:, 0:TG].rearrange("p (t o) -> p t o", o=1).to_broadcast([P, TG, D]), ALU.mult).then_inc(s["fin_x0"], 1)
            pool.wait_ge(s["fin_x0"], 1)
            nc.gpsimd.tensor_tensor(x_sb[:, 0:TG, :], xh_all[:, 0:TG, :], x_sb[:, 0:TG, :], ALU.add).then_inc(s["fin_x0"], 1)
            stored(1, 1)
            for t in range(TG, NT):
                gather(t, fin_y[(t - TG) // 4])

        @block.scalar
        def _(act):
            def copies(g):
                for n in range(4 * g, 4 * g + 4):
                    act.wait_ge(s["tr"], n + 1)
                    need(act, s["lg"], n - 1)
                    nc.scalar.activation(xhT[n % 2], (pA, pB)[n % 2][:], ACT.Copy).then_inc(s["trc"], 1)

            def exp_logits(n):
                act.wait_ge(s["diff"], n + 1)
                nc.scalar.activation(lexp[:], cand[:], ACT.Exp).then_inc(s["lexp"], 1)

            def experts(f):
                e = fs[f]

                def gelu(m, c):
                    t = 4 * m + c
                    act.wait_ge(e["up"], t + 1)
                    need(act, e["down"], t - 1)
                    for k in range(FC):
                        i = nc.scalar.activation(hT[c % 2][:, k, :], pE[:, (c % 2) * 512 + k * P:(c % 2) * 512 + (k + 1) * P],
                                                 ACT.Gelu, bias=w1_st[c % 4][:, F + k:F + k + 1])
                    i.then_inc(e["gelu"], 1)
                for c in range(2):
                    gelu(0, c)
                with act.Fori(0, 11) as m:
                    for c in range(2, 6):
                        gelu(m, c)

            for g in range(2):
                copies(g)
                exp_logits(g)
            experts(0)

            def copy_x(B):
                act.wait_ge(s["xt_ps"], at(B, 1, 1))
                need(act, s["v_ps"], at(B, 1, -3))
                nc.scalar.activation(xT[B[1] % 4][:], pB[:, 0:256], ACT.Copy).then_inc(s["xt_sb"], 1)

            def high(B):
                r = B[1] % 2
                act.wait_ge(s["qk_ps"], at(B, 1, 1))
                need(act, stack_w[r], half(B, 96))
                nc.scalar.activation(parts[r][:, 0, :, :], pA[:].rearrange("p (a t) -> p a t", a=2), ACT.Copy,
                                     scale=QK_SCALE).then_inc(s["hi"], 1)

            def copy_m(B):
                act.wait_ge(s["mt_ps"], at(B, 1, 1))
                need(act, max_w[B[1] % 2], half(B, 16))
                nc.scalar.activation(mT[B[1] % 2][:], pMT, ACT.Copy).then_inc(s["mt_sb"], 1)

            def exps(B, u):
                r = B[1] % 2
                act.wait_ge(s["e_ps"], at(B, 6, u + 1))
                if u == 0:
                    need(act, s["pv_ps"], at(B, 2, -2))
                dst = pt0[r][:, u, :, :, :] if u < 4 else pt1[r][:, u - 4, :, :, :]
                w = 256 if u < 4 else 128
                nc.scalar.activation(dst, pE[:].rearrange("p (a b t) -> p a b t", a=2, t=w), ACT.Exp).then_inc(s["e_sb"], 1)

            def copy_pv(B, k):
                act.wait_ge(s["pv_ps"], at(B, 2, k + 1))
                need(act, s["back_ps"], at(B, 2, k - 1))
                nc.scalar.activation(outT[k][:], pO[:], ACT.Copy).then_inc(s["pv_sb"], 1)

            def copy_o(B):
                act.wait_ge(s["ot_ps"], at(B, 1, 1))
                need(act, s["wo_ps"], at(B, 1, -1))
                nc.scalar.activation(oT[B[1] % 2][:], pC[:, 0:256], ACT.Copy).then_inc(s["ot_sb"], 1)

            for b in range(2):
                copy_x((0, b))
                high((0, b))
            copy_m((0, 0))

            def r_keep(B):
                act.wait_ge(s["r_xh"], at(B, 1, 1))
                nc.scalar.activation(xh_all[:, tiles(B), :], xr[B[1] % 2][:], ACT.Copy).then_inc(s["r_copied"], 1)

            def r_copy(B):
                act.wait_ge(s["r_tps"], at(B, 1, 1))
                need(act, s["r_lps"], at(B, 1))
                nc.scalar.activation(xrT[:], pA[:, 0:256], ACT.Copy).then_inc(s["r_tsb"], 1)

            def act_step(B):
                if has(B, 2):
                    copy_x(nxt(B, 2))
                    high(nxt(B, 2))
                if has(B, -3):
                    r_keep(nxt(B, -3))
                if has(B, 0):
                    exps(B, 0)
                if has(B, -2):
                    copy_o(nxt(B, -2))
                if has(B, 0):
                    exps(B, 1)
                    exps(B, 2)
                    exps(B, 3)
                if is_step(B, 12):
                    exp_logits(2)
                if has(B, 0):
                    exps(B, 4)
                if has(B, -3):
                    r_copy(nxt(B, -3))
                if has(B, -1):
                    copy_pv(nxt(B, -1), 0)
                if has(B, 1):
                    copy_m(nxt(B, 1))
                if has(B, 0):
                    exps(B, 5)
                if has(B, -1):
                    copy_pv(nxt(B, -1), 1)

            steps(act, act_step)
            exp_logits(3)
            experts(1)

        @block.tensor
        def _(pe):
            pe.wait_ge(s["load_c"], 48)

            def logits(g):
                def turn(n):
                    pe.wait_ge(s["xh"], n + 1)
                    need(pe, s["trc"], n - 1)
                    for j in range(4):
                        i = pe.transpose((pA, pB)[n % 2][:, j * P:(j + 1) * P], xh_all[:, 4 * n + j, :], ident_f)
                    i.then_inc(s["tr"], 1)

                turn(4 * g)
                for n in range(4 * g, 4 * g + 4):
                    if n < 4 * g + 3:
                        turn(n + 1)
                    pe.wait_ge(s["trc"], n + 1)
                    for j in range(4):
                        i = pe.matmul(pM[0][:, (4 * n + j) * NE:(4 * n + j + 1) * NE], xhT[n % 2][:, j * P:(j + 1) * P], wr_sb[:],
                                      start=True, stop=True)
                    i.then_inc(s["lg"], 1)

            def ranks(n, bank):
                pe.wait_ge(s["route"], n + 1)
                oh = onehot[:].rearrange("p e t -> p (e t)")
                pe.matmul(bank[:, 0:NE * TG], before, oh, start=True, stop=True)
                pe.matmul(bank[:, 256:256 + NE * TG], ones_b, oh, start=True, stop=True).then_inc(s["rank"], 1)

            def experts(f):
                e = fs[f]

                def turn(m, c):
                    t = 4 * m + c
                    pe.wait_ge(e["load"][c % 4], 16 * m + 16 * (c // 4 + 1))
                    need(pe, e["xTc"], t - 1)
                    pe.transpose((pA, pB)[c % 2][:, 0:P], xs[c % 4], ident_f).then_inc(e["xT"], 1)

                def up(m, c):
                    t = 4 * m + c
                    pe.wait_ge(e["w1c"], t + 1)
                    pe.wait_ge(e["xTc"], t + 1)
                    need(pe, e["gelu"], t - 1)
                    for k in range(FC):
                        i = pe.matmul(pE[:, (c % 2) * 512 + k * P:(c % 2) * 512 + (k + 1) * P],
                                      w1_st[c % 4][:, k * P:(k + 1) * P], xsT[c % 2], start=True, stop=True)
                    i.then_inc(e["up"], 1)

                def expert(m, c):
                    t = 4 * m + c
                    return pe.value_load(expert_i[0:1, bass.ds(t, 1)], min_val=0, max_val=NE - 1)

                def down(m, c, x):
                    t = 4 * m + c
                    pe.wait_ge(e["gelu"], t + 1)
                    need(pe, e["y"], t - 1)
                    for k in range(FC):
                        i = pe.matmul(pM[c % 2][:, 0:D], hT[c % 2][:, k, :],
                                      w2_sb[:, bass.ds(x, 1), k, :].rearrange("p o d -> p (o d)"), start=(k == 0), stop=(k == FC - 1))
                    i.then_inc(e["down"], 1)

                turn(0, 0)
                turn(0, 1)
                up(0, 0)

                def tile(m, c):
                    x = expert(m, c - 1)
                    turn(m, c + 1)
                    up(m, c)
                    down(m, c - 1, x)

                for c in range(1, 4):
                    tile(0, c)
                with pe.Fori(1, 11) as m:
                    for c in range(4):
                        tile(m, c)
                tile(0, NS - 2)
                x = expert(0, NS - 2)
                up(0, NS - 1)
                down(0, NS - 2, x)
                down(0, NS - 1, expert(0, NS - 1))

            for g in range(2):
                logits(g)
                ranks(g, pM[1])
            pe.wait_ge(s["load_w"], LOADED)
            experts(0)

            def turn_x(B):
                r = B[1] % 2
                pe.wait_ge(s["ln_xh"], at(B, 1, 1))
                if has(B, -2):
                    pe.wait_ge(s["mt_sb"], at(B, 1, -1))
                else:
                    need(pe, s["xt_sb"], at(B, 1))
                for j in range(2):
                    i = pe.transpose(pB[:, j * P:(j + 1) * P], xh[r][:, j, :], ident_f)
                i.then_inc(s["xt_ps"], 1)

            def project_qk(B):
                pe.wait_ge(s["xt_sb"], at(B, 1, 1))
                need(pe, s["rest"], at(B, 1))
                if has(B, -5):
                    need(pe, s["r_lg"], at(B, 1, -5))
                if is_step(B, 15):
                    pe.wait_ge(s["ranks_sb"], 3)
                for a in range(2):
                    i = pe.matmul(pA[:, a * 256:(a + 1) * 256], wqk_sb[:, a, :], xT[B[1] % 4][:], start=True, stop=True)
                i.then_inc(s["qk_ps"], 1)

            def project_v(B):
                if has(B, 2):
                    pe.wait_ge(s["xt_sb"], at(B, 1, 3))
                else:
                    pe.wait_ge(s["mt_sb"], at(B, 1, 1))
                for j in range(2):
                    i = pe.matmul(pB[:, 256 + j * P:256 + (j + 1) * P], xT[B[1] % 4][:, j * P:(j + 1) * P], wv_sb[:], start=True, stop=True)
                i.then_inc(s["v_ps"], 1)

            def maxima(B, u):
                r = B[1] % 4
                if u == 0:
                    pe.wait_ge(stack_r[r], quarter(B, 64, 64))
                if u < 4:
                    n, w, g0 = 2, 256, 2 * u
                else:
                    n, w, g0 = 4, 128, 4 * (u - 4)
                v = [bank[:].rearrange("p (n w) -> p n w", w=w) for bank in pM]
                q0 = 128 if u < 4 else 0
                for hh in range(2):
                    need(pe, s["m_neg"], at(B, 12, 2 * u + hh - 1))
                    pe.matmul(v[hh][:, :, w - 128:w], ident_b, mask_q.rearrange("p (o k) -> p o k", o=1).to_broadcast([P, n, P]),
                              start=True, stop=False, skip_group_check=True)
                for j in range(n):
                    for hh in range(2):
                        i = pe.matmul(v[hh][:, j, :], qs[r][hh * 64:hh * 64 + KM, g0 + j, q0:q0 + 128],
                                      ks[r][hh * 64:hh * 64 + KM, g0 + j, 0:w], start=False, stop=(j == n - 1), skip_group_check=True)
                        if j == n - 1:
                            i.then_inc(s["m_ps"], 1)

            def scores(B, u):
                r = B[1] % 4
                if u == 0:
                    pe.wait_ge(max_r[r], quarter(B, 32, 32))
                need(pe, s["e_sb"], at(B, 6, u))
                if u < 4:
                    n, w, g0, k0 = 2, 256, 2 * u, 0
                else:
                    n, w, g0, k0 = 4, 128, 4 * (u - 4), 128
                v = pE[:].rearrange("p (a n w) -> p a n w", a=2, w=w)
                for hh in range(2):
                    pe.matmul(v[:, hh, :, 0:128], ident_b, mask_k.rearrange("p (o k) -> p o k", o=1).to_broadcast([P, n, P]),
                              start=True, stop=False, skip_group_check=True)
                for j in range(n):
                    for hh in range(2):
                        i = pe.matmul(v[:, hh, j, :], ks[r][hh * 64:hh * 64 + KE, g0 + j, k0:k0 + 128],
                                      qs[r][hh * 64:hh * 64 + KE, g0 + j, 256 - w:256], start=False, stop=(j == n - 1), skip_group_check=True)
                i.then_inc(s["e_ps"], 1)

            def attend(B, u):
                r = B[1] % 2
                if u == 0:
                    pe.wait_ge(s["e_sb"], at(B, 6, 6))
                    pe.wait_ge(s["v_sb"], at(B, 1, 1))
                if u % 2 == 0:
                    need(pe, s["pv_sb"], at(B, 2, u // 2))
                for keys in range(2):
                    for j in range(4):
                        o = pO[32 * j:32 * j + VW, (u % 2) * 256 + keys * 128:(u % 2) * 256 + 256]
                        p = pt0[r][:, u, j % 2, j // 2, :] if keys == 0 else pt1[r][:, u // 2, j % 2, 2 * (u % 2) + j // 2, :]
                        i = pe.matmul(o, vaug[r][:, keys, 4 * u + j, :], p, start=(keys == 0), stop=(keys == 1), skip_group_check=True)
                if u % 2:
                    i.then_inc(s["pv_ps"], 1)

            def turn_back(B, k):
                pe.wait_ge(s["pv_sb"], at(B, 2, k + 1))
                if k == 0:
                    need(pe, s["x_attn"], at(B, 1))
                else:
                    pe.wait_ge(s["o_nrm"], at(B, 2, 1))
                for j in range(2):
                    for a in range(2):
                        i = pe.transpose(pC[:, j * 256 + a * P:j * 256 + (a + 1) * P], outT[k][:, a * 256 + j * P:a * 256 + (j + 1) * P], ident_f)
                i.then_inc(s["back_ps"], 1)

            def turn_m(B):
                r = B[1] % 2
                pe.wait_ge(s["m_split"], at(B, 1, 1))
                if has(B, -1):
                    pe.wait_ge(s["v_sb"], at(B, 1))
                else:
                    pe.wait_ge(s["xt_sb"], 2)
                alone(pe)
                for j in range(2):
                    i = pe.transpose(pMT[:, j * P:(j + 1) * P], mparts[r][:, j, :, :, :].rearrange("p a m g -> p (a m g)"), ident_b)
                i.then_inc(s["mt_ps"], 1)

            def turn_o(B):
                r = B[1] % 2
                pe.wait_ge(s["o_nrm"], at(B, 2, 2))
                for j in range(2):
                    i = pe.transpose(pC[:, j * P:(j + 1) * P], o_sb[r][:, j, :], ident_f)
                i.then_inc(s["ot_ps"], 1)

            def project_o(B):
                r = B[1] % 2
                pe.wait_ge(s["ot_sb"], at(B, 1, 1))
                for j in range(2):
                    i = pe.matmul(pC[:, 256 + j * P:256 + (j + 1) * P], oT[r][:, j * P:(j + 1) * P], wo_sb[:], start=True, stop=True)
                i.then_inc(s["wo_ps"], 1)

            def r_turn(B):
                pe.wait_ge(s["r_xh"], at(B, 1, 1))
                if has(B, 5):
                    pe.wait_ge(s["rest"], at(B, 1, 6))
                else:
                    pe.wait_ge(s["rest"], NB)
                    pe.wait_ge(s["r_lg"], at(B, 1))
                for j in range(2):
                    i = pe.transpose(pA[:, j * P:(j + 1) * P], xr[B[1] % 2][:, j, :], ident_f)
                i.then_inc(s["r_tps"], 1)

            def r_logits(B):
                pe.wait_ge(s["r_tsb"], at(B, 1, 1))
                for j in range(2):
                    i = pe.matmul(pA[:, 256 + j * NE:256 + (j + 1) * NE], xrT[:, j * P:(j + 1) * P], wr_sb[:], start=True, stop=True)
                i.then_inc(s["r_lps"], 1)

            for b in range(2):
                turn_x((0, b))
                project_qk((0, b))
            for u in range(6):
                maxima((0, 0), u)
            turn_m((0, 0))

            def pe_step(B):
                if has(B, 2):
                    turn_x(nxt(B, 2))
                if has(B, 1):
                    maxima(nxt(B, 1), 0)
                if has(B, -2):
                    turn_back(nxt(B, -2), 1)
                if has(B, 1):
                    maxima(nxt(B, 1), 1)
                if has(B, 2):
                    project_qk(nxt(B, 2))
                if has(B, 0):
                    scores(B, 0)
                if has(B, 1):
                    maxima(nxt(B, 1), 2)
                if has(B, -2):
                    turn_o(nxt(B, -2))
                if has(B, 0):
                    scores(B, 1)
                if has(B, 1):
                    maxima(nxt(B, 1), 3)
                if has(B, -2):
                    project_o(nxt(B, -2))
                if has(B, 0):
                    scores(B, 2)
                if has(B, 1):
                    maxima(nxt(B, 1), 4)
                if has(B, 0):
                    project_v(B)
                    scores(B, 3)
                if has(B, 1):
                    maxima(nxt(B, 1), 5)
                if has(B, -1):
                    attend(nxt(B, -1), 0)
                if has(B, 0):
                    scores(B, 4)
                if has(B, -3):
                    r_turn(nxt(B, -3))
                if has(B, -1):
                    attend(nxt(B, -1), 1)
                if has(B, 1):
                    turn_m(nxt(B, 1))
                if has(B, 0):
                    scores(B, 5)
                if has(B, -1):
                    turn_back(nxt(B, -1), 0)
                if has(B, -3):
                    r_logits(nxt(B, -3))
                if has(B, -1):
                    attend(nxt(B, -1), 2)
                    attend(nxt(B, -1), 3)
                if is_step(B, 12):
                    pe.wait_ge(s["r_lg"], 10)
                    ranks(2, pA)

            steps(pe, pe_step)
            ranks(3, pM[1])
            experts(1)

        @block.vector
        def _(dve):
            V = nc.vector

            link = [0]

            def then(ins):
                link[0] += 1
                ins.then_inc(s["chain"], 1)
                dve.wait_ge(s["chain"], link[0])

            def moments(g):
                t0, t1 = TG * g, TG * g + TG
                for q in range(2 * g, 2 * g + 2):
                    dve.wait_ge(load_x[q], 16)
                    for t in range(8 * q, 8 * q + 8):
                        i = V.bn_stats(st_all[:, t, :], x_sb[:, t, :])
                then(i)
                me, mo, ve, vo = (st_all[:, t0:t1, k] for k in (1, 4, 2, 5))
                V.tensor_tensor(mean_all[:, t0:t1], me, mo, ALU.add)
                V.tensor_tensor(ln_a[:], me, mo, ALU.subtract)
                then(V.tensor_tensor(ln_b[:], ve, vo, ALU.add))
                then(V.scalar_tensor_tensor(ln_c[:, t0:t1], ln_a[:], 0.25, ln_a[:], ALU.mult, ALU.mult))
                then(V.scalar_tensor_tensor(ln_a[:], ln_b[:], 1.0 / D, ln_c[:, t0:t1], ALU.mult, ALU.add))
                V.tensor_scalar(ln_c[:, t0:t1], ln_a[:], EPS, None, ALU.add).then_inc(s["lnst"], 1)
                then(V.tensor_scalar(mean_all[:, t0:t1], mean_all[:, t0:t1], 0.5, None, ALU.mult))

            def normed(g):
                dve.wait_ge(s["lnpow"], g + 1)
                for t in range(TG * g, TG * g + TG):
                    i = V.tensor_scalar(xh_all[:, t, :], x_sb[:, t, :], mean_all[:, t:t + 1], rstd_all[:, t:t + 1],
                                        ALU.subtract, ALU.mult)
                    if t % 4 == 3:
                        i.then_inc(s["xh"], 1)

            def per_tile(a):
                return a.rearrange("p (t o) -> p t o", o=1).to_broadcast([P, TG, NE])

            def choose(n):
                g = n % 2
                lg = lg_all[:, TG * g:TG * g + TG, :]
                if n < 2:
                    dve.wait_ge(s["lg"], 4 * (g + 1))
                    then(V.tensor_copy(lg, pM[0][:, TG * NE * g:TG * NE * (g + 1)].rearrange("p (t e) -> p t e", e=NE)))
                else:
                    dve.wait_ge(s["r_lg"], 8 * (g + 1))
                then(V.tensor_reduce(lmax[:], lg, AX.X, ALU.max))
                V.tensor_tensor(cand[:], lg, per_tile(lmax[:]), ALU.subtract).then_inc(s["diff"], 1)
                dve.wait_ge(s["diff"], n + 1)
                then(V.tensor_scalar(equal[:], cand[:], 0.0, None, ALU.is_equal))
                then(V.tensor_tensor(equal[:], equal[:], rank8.rearrange("p (o e) -> p o e", o=1).to_broadcast([P, TG, NE]), ALU.mult))
                then(V.tensor_reduce(chosen[:], equal[:], AX.X, ALU.max))
                V.tensor_tensor(onehot[:], rank8.rearrange("p (e o) -> p e o", o=1).to_broadcast([P, NE, TG]),
                                chosen[:].rearrange("p (o t) -> p o t", o=1).to_broadcast([P, NE, TG]), ALU.is_equal).then_inc(s["route"], 1)
                dve.wait_ge(s["lexp"], n + 1)
                then(V.tensor_reduce(lmax[:], lexp[:], AX.X, ALU.add))
                then(V.reciprocal(lmax[:], lmax[:]))
                then(V.tensor_scalar(pmax[:, TG * g:TG * g + TG], lmax[:], 0.5, None, ALU.mult))

            def places(n, bank):
                g = n % 2
                dve.wait_ge(s["rank"], n + 1)
                rank = bank[:, 0:NE * TG].rearrange("p (e t) -> p e t", e=NE)
                total = bank[:, 256:256 + NE * TG].rearrange("p (e t) -> p e t", e=NE)
                V.tensor_copy(place[:], rank)
                V.tensor_copy(fills[:], total).then_inc(s["ranks_sb"], 1)
                dve.wait_ge(s["ranks_sb"], n + 1)
                then(V.tensor_tensor_scan(upto[:].rearrange("p e t -> p (e t)"), keep, fills[:].rearrange("p e t -> p (e t)"),
                                          0.0, ALU.mult, ALU.add))
                then(V.tensor_tensor(place[:], place[:], upto[:], ALU.add))
                then(V.tensor_tensor(place[:], place[:], fills[:], ALU.subtract))
                then(V.tensor_tensor(fills[:], upto[:, :, TG - 1:TG].to_broadcast([P, NE, TG]),
                                     steps128.rearrange("p (o t) -> p o t", o=1).to_broadcast([P, NE, TG]), ALU.is_gt))
                then(V.tensor_reduce(ntiles[:], fills[:], AX.X, ALU.add))
                then(V.tensor_tensor_scan(tile_end[:], ones8, ntiles[:], 0.0, ALU.mult, ALU.add))
                then(V.tensor_tensor(tile_start[:], tile_end[:], ntiles[:], ALU.subtract))
                then(V.tensor_scalar(tile_start[:], tile_start[:], float(P), None, ALU.mult))
                then(V.tensor_tensor(place[:], place[:], tile_start[:].rearrange("p (e o) -> p e o", o=1).to_broadcast([P, NE, TG]), ALU.add))
                then(V.tensor_tensor(place[:], place[:], onehot[:], ALU.mult))
                then(V.tensor_reduce(slot_f[:], place[:].rearrange("p e t -> p t e"), AX.X, ALU.add))
                V.tensor_copy(slot_i[:, TG * g:TG * g + TG], slot_f[:]).then_inc(s["place"], 1)
                then(V.tensor_tensor(expert_cmp[:], slot_ids.rearrange("p (s o) -> p s o", o=1).to_broadcast([P, NSG, NE - 1]),
                                     tile_end[:, 0:NE - 1].rearrange("p (o e) -> p o e", o=1).to_broadcast([P, NSG, NE - 1]), ALU.is_ge))
                then(V.tensor_reduce(expert_f[:], expert_cmp[:], AX.X, ALU.add))
                V.tensor_copy(expert_i[:, NSG * g:NSG * g + NSG], expert_f[:]).then_inc(s["ts"], 1)

            def experts(f):
                e = fs[f]

                def copy_w1(m, c):
                    t = 4 * m + c
                    x = dve.value_load(expert_i[0:1, bass.ds(t, 1)], min_val=0, max_val=NE - 1)
                    need(dve, e["gelu"], t - 3)
                    need(dve, e["y"], t - 3)
                    V.tensor_copy(w1_st[c % 4], w1_sb[:, bass.ds(x, 1), :].rearrange("p o n -> p (o n)")).then_inc(e["w1c"], 1)

                def copy_x(m, c):
                    t = 4 * m + c
                    dve.wait_ge(e["xT"], t + 1)
                    need(dve, e["up"], t - 1)
                    V.tensor_copy(xsT[c % 2], (pA, pB)[c % 2][:, 0:P]).then_inc(e["xTc"], 1)

                def add_bias(m, c):
                    t = 4 * m + c
                    if not isinstance(m, int) or c >= 4:
                        dve.wait_ge(e["store"][c % 4], 16 * m + 16 * (c // 4))
                    dve.wait_ge(e["down"], t + 1)
                    V.tensor_tensor(ys[c % 4], pM[c % 2][:, 0:D], w1_st[c % 4][:, F + FC:W1W], ALU.add).then_inc(e["y"], 1)

                if f == 1:
                    dve.wait_ge(s["pv_ps"], 2 * NB)
                dve.wait_ge(s["ts"], 2 * f + 2)
                for c in range(3):
                    copy_w1(0, c)
                copy_x(0, 0)
                copy_x(0, 1)
                for c in range(7):
                    copy_x(0, c + 2)
                    copy_w1(0, c + 3)
                    add_bias(0, c)
                with dve.Fori(1, 10) as m:
                    for c in range(3, 7):
                        copy_x(m, c + 2)
                        copy_w1(m, c + 3)
                        add_bias(m, c)
                copy_x(0, NS - 1)
                add_bias(0, NS - 3)
                add_bias(0, NS - 2)
                add_bias(0, NS - 1)

            moments(0)
            moments(1)
            for g in range(2):
                normed(g)
                choose(g)
                places(g, pM[1])
            dve.wait_ge(s["load_w"], LOADED)
            for r in range(2):
                i = V.memset(vaug[r][:], 1.0)
                i.then_inc(s["attn_vones"], 1)
            dve.wait_ge(s["attn_vones"], 2)
            experts(0)

            def residual(B):
                r = B[1] % 2
                if isinstance(B[0], int) and B[1] in (0, 8):
                    dve.wait_ge(got_y[B[1] // 8], 16 * TG)
                if not isinstance(B[0], int) and B[1] == 4:
                    dve.wait_ge(got_y[1], 16 * TG)
                for j in range(2):
                    t = at(B, 2, j)
                    xt = x_sb[:, bass.ds(t, 1), :].rearrange("p o d -> p (o d)")
                    i = V.scalar_tensor_tensor(xt, xh_all[:, bass.ds(t, 1), :].rearrange("p o d -> p (o d)"), pmax[:, bass.ds(t, 1)], xt, ALU.mult, ALU.add)
                i.then_inc(s["res_x"], 1)
                dve.wait_ge(s["res_x"], at(B, 1, 1))
                alone(dve)
                for j in range(2):
                    t = at(B, 2, j)
                    i = V.bn_stats(st2[r][:, j, :], x_sb[:, bass.ds(t, 1), :].rearrange("p o d -> p (o d)"))
                i.then_inc(s["stats"], 1)
                dve.wait_ge(s["stats"], at(B, 1, 1))
                need(dve, s["veps"], at(B, 1, -1))
                alone(dve)
                for j in range(2):
                    i = V.bn_aggr(mv[r][:, j, :], st2[r][:, j, :])
                i.then_inc(s["aggr"], 1)

            def norm_x(B):
                r = B[1] % 2
                dve.wait_ge(s["ln_pow"], at(B, 1, 1))
                need(dve, s["xt_ps"], at(B, 1, -1))
                for j in range(2):
                    t = at(B, 2, j)
                    i = V.tensor_scalar(xh[r][:, j, :], x_sb[:, bass.ds(t, 1), :].rearrange("p o d -> p (o d)"), mv[r][:, j, 0:1],
                                        rstd[r][:, j:j + 1], ALU.subtract, ALU.mult)
                i.then_inc(s["ln_xh"], 1)

            def middle(B):
                r = B[1] % 2
                dve.wait_ge(s["hi"], at(B, 1, 1))
                need(dve, s["lo"], at(B, 1))
                V.scalar_tensor_tensor(rest[:].rearrange("p (a t) -> p a t", a=2), pA[:].rearrange("p (a t) -> p a t", a=2),
                                       QK_SCALE, parts[r][:, 0, :, :], ALU.mult, ALU.subtract).then_inc(s["rest"], 1)
                dve.wait_ge(s["rest"], at(B, 1, 1))
                V.tensor_copy(parts[r][:, 1, :, :], rest[:].rearrange("p (a t) -> p a t", a=2)).then_inc(s["mid"], 1)

            def copy_v(B):
                r = B[1] % 2
                dve.wait_ge(s["v_ps"], at(B, 1, 1))
                need(dve, s["pv_ps"], at(B, 2, -2))
                V.tensor_copy(vaug[r][:, :, :, 0:HD], pB[:, 256:512].rearrange("p (a h d) -> p a h d", a=2, d=HD)).then_inc(s["v_sb"], 1)

            def m_reduce(B, u):
                r = B[1] % 2
                dve.wait_ge(s["m_ps"], at(B, 12, u + 1))
                if u == 0:
                    need(dve, s["mchain"], at(B, 3, -3))
                hh = u % 2
                if u < 8:
                    n, w, g0, blk = 2, 256, 2 * (u // 2), 1
                else:
                    n, w, g0, blk = 4, 128, 4 * ((u - 8) // 2), 0
                V.tensor_reduce(nmax[r][:, blk, hh, g0:g0 + n], pM[u % 2][:].rearrange("p (n w) -> p n w", w=w), AX.X, ALU.max,
                                negate=True).then_inc(s["m_neg"], 1)

            def m_split(B):
                r = B[1] % 2
                hi, mid, lo = (mparts[r][:, :, :, k, :].rearrange("p b a g -> p (b a) g") for k in range(3))
                nm = nmax[r][:].rearrange("p b a g -> p (b a) g")
                nr = nrest[:].rearrange("p b a g -> p (b a) g")
                dve.wait_ge(s["m_neg"], at(B, 12, 12))
                need(dve, s["mt_ps"], at(B, 1, -1))
                V.tensor_copy(hi, nm).then_inc(s["mchain"], 1)
                dve.wait_ge(s["mchain"], at(B, 3, 1))
                V.tensor_tensor(nr, nm, hi, ALU.subtract).then_inc(s["mchain"], 1)
                dve.wait_ge(s["mchain"], at(B, 3, 2))
                V.tensor_copy(mid, nr).then_inc(s["mchain"], 1)
                dve.wait_ge(s["mchain"], at(B, 3, 3))
                V.tensor_tensor(lo, nr, mid, ALU.subtract).then_inc(s["m_split"], 1)

            def norm_o(B, k):
                r = B[1] % 2
                v = pC[:].rearrange("p (j h w) -> p j h w", j=2, w=VW)
                dve.wait_ge(s["back_ps"], at(B, 2, k + 1))
                need(dve, s["o_nrm"], at(B, 2, k))
                V.reciprocal(rec[:], v[:, :, :, HD]).then_inc(s["o_rec"], 1)
                dve.wait_ge(s["o_rec"], at(B, 2, k + 1))
                if k == 0:
                    need(dve, s["ot_ps"], at(B, 1, -1))
                V.tensor_tensor(o_sb[r][:, :, 64 * k:64 * k + 64].rearrange("p j (h d) -> p j h d", d=HD), v[:, :, :, 0:HD],
                                rec[:].rearrange("p j (h o) -> p j h o", o=1).to_broadcast([P, 2, 8, HD]), ALU.mult).then_inc(s["o_nrm"], 1)

            def add_attn(B):
                dve.wait_ge(s["wo_ps"], at(B, 1, 1))
                xt = x_sb[:, tiles(B), :].rearrange("p a d -> p (a d)")
                V.tensor_tensor(xt, pC[:, 256:512], xt, ALU.add).then_inc(s["x_attn"], 1)

            residual((0, 0))
            residual((0, 1))
            norm_x((0, 0))
            norm_x((0, 1))
            middle((0, 0))
            middle((0, 1))
            residual((0, 2))
            norm_x((0, 2))
            for u in range(12):
                m_reduce((0, 0), u)
            m_split((0, 0))

            def r_stats(B):
                r = B[1] % 2
                dve.wait_ge(s["x_attn"], at(B, 1, 1))
                alone(dve)
                for j in range(2):
                    i = V.bn_stats(st3[r][:, j, :], x_sb[:, bass.ds(at(B, 2, j), 1), :].rearrange("p o d -> p (o d)"))
                i.then_inc(s["r_stats"], 1)
                dve.wait_ge(s["r_stats"], at(B, 1, 1))
                need(dve, s["r_veps"], at(B, 1, -1))
                alone(dve)
                for j in range(2):
                    i = V.bn_aggr(mv3[r][:, j, :], st3[r][:, j, :])
                i.then_inc(s["r_aggr"], 1)

            def r_norm(B):
                r = B[1] % 2
                dve.wait_ge(s["r_pow"], at(B, 1, 1))
                need(dve, s["r_tps"], at(B, 1, -1))
                need(dve, s["r_copied"], at(B, 1, -1))
                for j in range(2):
                    i = V.tensor_scalar(xr[r][:, j, :], x_sb[:, bass.ds(at(B, 2, j), 1), :].rearrange("p o d -> p (o d)"), mv3[r][:, j, 0:1],
                                        rstd3[r][:, j:j + 1], ALU.subtract, ALU.mult)
                i.then_inc(s["r_xh"], 1)

            def r_keep_logits(B):
                dve.wait_ge(s["r_lps"], at(B, 1, 1))
                V.tensor_copy(lg_all[:, tiles(B), :], pA[:, 256:256 + 2 * NE].rearrange("p (a e) -> p a e", e=NE)).then_inc(s["r_lg"], 1)

            def dve_step(B):
                if has(B, 1):
                    m_reduce(nxt(B, 1), 0)
                    m_reduce(nxt(B, 1), 1)
                if has(B, -2):
                    norm_o(nxt(B, -2), 1)
                if has(B, 1):
                    m_reduce(nxt(B, 1), 2)
                    m_reduce(nxt(B, 1), 3)
                if has(B, 2):
                    middle(nxt(B, 2))
                if has(B, 1):
                    m_reduce(nxt(B, 1), 4)
                    m_reduce(nxt(B, 1), 5)
                    m_reduce(nxt(B, 1), 6)
                    m_reduce(nxt(B, 1), 7)
                if has(B, -2):
                    add_attn(nxt(B, -2))
                if has(B, 3):
                    residual(nxt(B, 3))
                if has(B, -2):
                    r_stats(nxt(B, -2))
                if has(B, 1):
                    m_reduce(nxt(B, 1), 8)
                    m_reduce(nxt(B, 1), 9)
                if has(B, 0):
                    copy_v(B)
                if has(B, 1):
                    m_reduce(nxt(B, 1), 10)
                    m_reduce(nxt(B, 1), 11)
                    m_split(nxt(B, 1))
                if has(B, 3):
                    norm_x(nxt(B, 3))
                if is_step(B, 12):
                    choose(2)
                if has(B, -1):
                    norm_o(nxt(B, -1), 0)
                if has(B, -3):
                    r_keep_logits(nxt(B, -3))
                if has(B, -2):
                    r_norm(nxt(B, -2))
                if is_step(B, 12):
                    places(2, pA)

            steps(dve, dve_step)
            choose(3)
            places(3, pM[1])
            experts(1)
            for k in range(4):
                dve.wait_ge(fin_y[k], 64)
                for t in range(TG + 4 * k, TG + 4 * k + 4):
                    i = V.scalar_tensor_tensor(x_sb[:, t, :], xh_all[:, t, :], pmax[:, t:t + 1], x_sb[:, t, :], ALU.mult, ALU.add)
                i.then_inc(s["fin_x"], 1)


def kernel(L0_attn_x, L0_attn_Wq, L0_attn_Wk, L0_attn_Wv, L0_attn_Wo, L0_ffn_Wr, L0_ffn_W1, L0_ffn_b1, L0_ffn_W2, L0_ffn_b2):
    import numpy as np
    import concourse.bacc as bacc
    from concourse.bass_utils import run_bass_kernel_spmd

    f32 = np.float32
    bf16 = mybir.dt.np(BF16) if hasattr(mybir.dt, "np") else __import__("ml_dtypes").bfloat16
    c = np.ascontiguousarray

    w1b = np.concatenate([L0_ffn_W1, L0_ffn_b1.reshape(NE, FC, P).transpose(0, 2, 1),
                          np.broadcast_to(L0_ffn_b2[:, None, :], (NE, P, D))], axis=2)
    order = np.array([(2 * g + hh) * HD + d for hh in range(2) for d in range(HD) for g in range(8)])

    cf = np.zeros((P, 512), f32)
    cf[:, 0:128] = np.eye(P)
    cf[:, 128:128 + TG] = np.arange(TG) * P
    cf[:, 160:160 + NE * TG] = (np.arange(NE * TG) % TG != 0)
    cf[:, 416:424] = 8 - np.arange(8)
    cf[:, 424:424 + NSG] = np.arange(NSG)
    cf[:, 464:472] = 1
    cf[:, 472:504] = -0.5
    i = np.arange(P)
    cb = np.zeros((P, 640), f32)
    cb[:, 0:128] = np.eye(P)
    cb[:, 128:256] = i[:, None] < i[None, :]
    cb[:, 256:384] = 1
    cb[:, 384:512] = np.where(i[None, :] > i[:, None], -1e30, 0)
    cb[:, 512:640] = np.where(i[:, None] > i[None, :], -1e30, 0)

    def three(a):
        hi = a.astype(bf16)
        mid = (a - hi.astype(np.float64)).astype(bf16)
        lo = (a - hi.astype(np.float64) - mid.astype(np.float64)).astype(bf16)
        return hi, mid, lo

    base = 2.0 ** (-8.0 / H)
    slopes = np.array([base ** n for n in range(1, H + 1)], dtype=f32).astype(np.float64)
    qconst = np.ones((2, 6, 8, 256), bf16)
    kconst = np.ones((2, 9, 8, 256), bf16)
    for hh in range(2):
        for g in range(8):
            bias = three(slopes[2 * g + hh] * (np.arange(256) - 128.0))
            for n in range(3):
                kconst[hh, n, g] = bias[n]
                qconst[hh, 3 + n, g] = -bias[n]

    arrays = {
        "x": c(L0_attn_x.reshape(NT * P, D)), "w1b": c(w1b), "w2": c(L0_ffn_W2),
        "wr": c(L0_ffn_Wr),
        "wq": c(L0_attn_Wq[order].T), "wk": c(L0_attn_Wk[order].T), "wv": c(L0_attn_Wv.T), "wo": c(L0_attn_Wo.T),
        "cf": cf, "cb": cb.astype(bf16), "qconst": qconst, "kconst": kconst,
    }
    nc = bacc.Bacc("TRN2", target_bir_lowering=False, num_devices=1)
    args = []
    for name, a in arrays.items():
        args.append(nc.dram_tensor(f"in_{name}", a.shape, mybir.dt.from_np(a.dtype), kind="ExternalInput").ap())
    out = nc.dram_tensor("out", (NT * P, D), F32, kind="ExternalOutput").ap()
    build(nc, *args, out)
    r = run_bass_kernel_spmd(nc, [{f"in_{n}": a for n, a in arrays.items()}], core_ids=[0])
    return r.results[0]["out"].reshape(NB, 256, D)
```

```python
from contextlib import ExitStack

import concourse.bass as bass
from concourse import mybir

P = 128
NB = 16
NT = 32
D = 128
H = 16
HD = 8
NE = 8
F = 512
FC = F // P
GT = ((12, 20), (20, 12))
T0 = tuple((0, g[0]) for g in GT)
NSG = tuple(tuple(n + NE - 1 for n in g) for g in GT)
NS = NT + 2 * (NE - 1)
NSM = tuple(max(NSG[0][g], NSG[1][g]) for g in range(2))
TM = max(GT[0] + GT[1])
SM = max(NSM)
EPS = 1e-5
W1W = F + FC + D
VW = 32
SPLIT = 6 * HD
KM = SPLIT + 6
KE = SPLIT + 9
PT0 = H * 256
PT1 = H * 128
QK_SCALE = float(HD) ** -0.25
GROUPS = GT[0] + GT[1]
C_STEPS = P
C_KEEP = tuple(C_STEPS + TM + NE * sum(GROUPS[:n]) for n in range(4))
C_RANK = C_KEEP[3] + NE * GROUPS[3]
C_IDS = C_RANK + NE
C_ONES = C_IDS + SM
C_HALF = C_ONES + NE
C_END = C_HALF + NT

ALU = mybir.AluOpType
ACT = mybir.ActivationFunctionType
AX = mybir.AxisListType
F32 = mybir.dt.float32
BF16 = mybir.dt.bfloat16
I32 = mybir.dt.int32


def build(nc, x, w1b, w2, wr, wq, wk, wv, wo, cf, cb, qconst, kconst, out):
    ctx = ExitStack()
    with ctx:
        def sb(name, shape, dt=F32):
            return ctx.enter_context(nc.sbuf_tensor(name, shape, dt))

        def psum(name, shape, dt=F32):
            return ctx.enter_context(nc.psum_tensor(name, shape, dt))

        def sem(name):
            return ctx.enter_context(nc.semaphore(name))

        def dram(name, shape, dt=F32):
            return nc.dram_tensor(name, shape, dt, kind="Internal").ap()

        slot_x = [dram(f"slot_x{g}", [NSM[g] * P, D]) for g in range(2)]
        slot_y = [dram(f"slot_y{g}", [NSM[g] * P, D]) for g in range(2)]
        stack_q = [dram(f"stack_q{r}", [6, P, 256], BF16) for r in range(2)]
        stack_k = [dram(f"stack_k{r}", [6, P, 256], BF16) for r in range(2)]
        max_d = [dram(f"max_d{r}", [48, 256], BF16) for r in range(2)]

        x_sb = sb("x_sb", [P, NT, D])
        w1_sb = sb("w1_sb", [P, NE, W1W])
        w2_sb = sb("w2_sb", [P, NE, FC, D])
        wr_sb = sb("wr_sb", [P, NE])
        wqk_sb = sb("wqk_sb", [P, 2, D])
        wv_sb = sb("wv_sb", [P, D])
        wo_sb = sb("wo_sb", [P, D])
        cf_sb = sb("cf_sb", [P, cf.shape[1]])
        cb_sb = sb("cb_sb", [P, cb.shape[1]], BF16)
        ident_f = cf_sb[:, 0:P]
        steps128 = cf_sb[:, C_STEPS:C_STEPS + TM]
        keep = [cf_sb[:, C_KEEP[n]:C_KEEP[n] + NE * GROUPS[n]] for n in range(4)]
        rank8 = cf_sb[:, C_RANK:C_RANK + NE]
        slot_ids = cf_sb[:, C_IDS:C_IDS + SM]
        ones8 = cf_sb[:, C_ONES:C_ONES + NE]
        minus_half = cf_sb[:, C_HALF:C_END]
        ident_b = cb_sb[:, 0:128]
        before = cb_sb[:, 128:256]
        ones_b = cb_sb[:, 256:384]
        mask_q = cb_sb[:, 384:512]
        mask_k = cb_sb[:, 512:640]

        xh_all = sb("xh_all", [P, NT, D])
        st_all = sb("st_all", [P, NT, 6])
        ln_a = sb("ln_a", [P, TM])
        ln_b = sb("ln_b", [P, TM])
        ln_c = sb("ln_c", [P, NT])
        mean_all = sb("mean_all", [P, NT])
        rstd_all = sb("rstd_all", [P, NT])
        lg_all = sb("lg_all", [P, NT, NE])
        lmax = sb("lmax", [P, TM])
        lexp = sb("lexp", [P, TM, NE])
        cand = sb("cand", [P, TM, NE])
        equal = sb("equal", [P, TM, NE])
        chosen = sb("chosen", [P, TM])
        onehot = sb("onehot", [P, NE * TM], BF16)
        upto = sb("upto", [P, NE * TM])
        place = sb("place", [P, NE * TM])
        fills = sb("fills", [P, NE * TM])
        ntiles = sb("ntiles", [P, NE])
        tile_end = sb("tile_end", [P, NE])
        tile_start = sb("tile_start", [P, NE])
        expert_cmp = sb("expert_cmp", [P, SM, NE - 1])
        expert_f = sb("expert_f", [P, SM])
        expert_i = sb("expert_i", [P, NS], I32)
        slot_f = sb("slot_f", [P, TM])
        slot_i = sb("slot_i", [P, NT], I32)
        pmax = sb("pmax", [P, NT])
        st3 = [sb(f"st3{r}", [P, 2, 6]) for r in range(2)]
        mv3 = [sb(f"mv3{r}", [P, 2, 2]) for r in range(2)]
        veps3 = [sb(f"veps3{r}", [P, 2]) for r in range(2)]
        rstd3 = [sb(f"rstd3{r}", [P, 2]) for r in range(2)]
        xr = [sb(f"xr{r}", [P, 2, D]) for r in range(2)]
        xrT = sb("xrT", [P, 256])
        region = [sb(f"region{r}", [P, PT0 + PT1]) for r in range(2)]
        pt0 = [a[:, 0:PT0].rearrange("p (u a b t) -> p u a b t", u=4, a=2, b=2) for a in region]
        pt1 = [a[:, PT0:].rearrange("p (u a b t) -> p u a b t", u=2, a=2, b=4) for a in region]
        zeros = region[1][:, 0:SM * P].rearrange("p (a b) -> p a b", b=P)
        xhT = [region[1][:, 4096 + r * 512:4608 + r * 512] for r in range(2)]
        space = [0]

        def carve(width):
            space[0] += width
            return region[0][:, space[0] - width:space[0]]
        w1_st = [carve(W1W) for r in range(4)]
        xs = [carve(D) for r in range(4)]
        hT = [carve(F).rearrange("p (k t) -> p k t", k=FC) for r in range(2)]
        xsT = [carve(P) for r in range(2)]
        ys = [carve(D) for r in range(4)]
        st2 = [sb(f"st2{r}", [P, 2, 6]) for r in range(2)]
        mv = [sb(f"mv{r}", [P, 2, 2]) for r in range(2)]
        veps = [sb(f"veps{r}", [P, 2]) for r in range(2)]
        rstd = [sb(f"rstd{r}", [P, 2]) for r in range(2)]
        xh = [sb(f"xh{r}", [P, 2, D]) for r in range(2)]
        xT = [sb(f"xT{r}", [P, 256]) for r in range(4)]
        rest = sb("rest", [P, 512])
        parts = [sb(f"parts{r}", [P, 3, 2, 256], BF16) for r in range(2)]
        qs = [sb(f"qs{r}", [P, 8, 256], BF16) for r in range(4)]
        ks = [sb(f"ks{r}", [P, 8, 256], BF16) for r in range(4)]
        vaug = [sb(f"vaug{r}", [P, 2, H, VW]) for r in range(2)]
        nmax = [sb(f"nmax{r}", [P, 2, 2, 8]) for r in range(2)]
        nrest = sb("nrest", [P, 2, 2, 8])
        mparts = [sb(f"mparts{r}", [P, 2, 2, 3, 8], BF16) for r in range(2)]
        mT = [sb(f"mT{r}", [48, 256], BF16) for r in range(2)]
        outT = [sb(f"outT{r}", [P, 512]) for r in range(2)]
        rec = sb("rec", [P, 2, 8])
        o_sb = [sb(f"o_sb{r}", [P, 2, D]) for r in range(2)]
        oT = [sb(f"oT{r}", [P, 256]) for r in range(2)]

        pE = psum("pE", [P, 1024])
        pMM = psum("pM", [P, 1024])
        pM = [pMM[:, 0:512], pMM[:, 512:1024]]
        pA = psum("pA", [P, 512])
        pB = psum("pB", [P, 512])
        pO = psum("pO", [P, 512])
        pC = psum("pC", [P, 512])
        pMT = pB[0:48, 0:128].bitcast(BF16)
        pMT_early = pC[0:48, 0:128].bitcast(BF16)
        ROWS_SOON = 6
        ROWS = GT[0][1] // 4
        EARLY = 24

        names = """load_w load_e load_c zeroed attn_vones
            hi rest mid lo v_ps v_sb xt_ps xt_sb qk_ps ln_pow ln_xh
            m_ps m_neg m_split mt_ps mt_sb e_ps e_sb pv_ps pv_sb back_ps o_rec o_nrm ot_ps ot_sb wo_ps x_attn
            res_x stats aggr veps mchain
            r_stats r_aggr r_veps r_pow r_xh r_copied r_tps r_tsb r_lps r_lg
            lnst lnpow xh tr trc lg chain diff lexp route rank ranks_sb place ts fin_x fin_x0""".split()
        s = {n: sem(n) for n in names}
        waited = sem("waited")
        load_x = [sem(f"load_x{q}") for q in range(4)]
        slots_clear = [sem(f"slots_clear{g}") for g in range(2)]
        got_y = [sem(f"got_y{k}") for k in range(6)]
        stack_w = [sem(f"stack_w{r}") for r in range(2)]
        stack_r = [sem(f"stack_r{r}") for r in range(4)]
        stack_w_pool, stack_r_pool = sem("stack_w_pool"), sem("stack_r_pool")
        max_w = [sem(f"max_w{r}") for r in range(2)]
        max_r = [sem(f"max_r{r}") for r in range(4)]
        fs = []
        for f in range(2):
            e = {n: sem(f"{n}{f}") for n in "w1c xT xTc up gelu down y".split()}
            e["scattered"] = [sem(f"scattered{f}_{g}") for g in range(2)]
            e["load"] = [sem(f"ld{f}_{r}") for r in range(4)]
            e["store"] = [sem(f"sto{f}_{r}") for r in range(4)]
            fs.append(e)
        fin_y = [sem(f"fin_y{k}") for k in range(5)]
        fin_o = sem("fin_o")

        LOADED = 16 * (4 + 4 * 2 * 2)

        block = ctx.enter_context(nc.Block())

        def at(B, per, more=0):
            m, c = B
            return per * c + more if isinstance(m, int) else m * (4 * per) + (per * c + more)

        def half(B, per, more=0):
            m, c = B
            return per * (c // 2) + more if isinstance(m, int) else m * (2 * per) + (per * (c // 2) + more)

        def quarter(B, per, more=0):
            m, c = B
            return per * (c // 4) + more if isinstance(m, int) else m * per + (per * (c // 4) + more)

        def nxt(B, d):
            return (B[0], B[1] + d)

        def need(eng, semaphore, value):
            if isinstance(value, int) and value <= 0:
                return
            eng.wait_ge(semaphore, value)

        def alone(eng):
            eng.sem_inc(waited, 1)

        def steps(eng, step):
            for c in range(4):
                step((0, c))
            with eng.Fori(1, 3) as m:
                for c in range(4):
                    step((m, c))
            for c in range(12, NB):
                step((0, c))

        def written(B):
            if is_step(B, 1):
                return stack_w_pool, 96
            return (stack_w[1], half(B, 96)) if B[1] % 2 else (stack_w[0], half(B, 96, 96))

        def read_back(B):
            if is_step(B, 1):
                return stack_r_pool, 64
            return (stack_r[1], quarter(B, 64)) if B[1] % 4 == 1 else (stack_r[B[1] % 4], quarter(B, 64, 64))

        def is_step(B, c):
            return isinstance(B[0], int) and B[1] == c

        def has(B, d):
            return not isinstance(B[0], int) or 0 <= B[1] + d < NB

        def score_banks(B, u):
            return pMM[:] if is_step(B, NB - 1) and u % 2 else pE[:]

        def tiles(B):
            return bass.ds(at(B, 2), 2)

        def stack_write(eng, B):
            r = B[1] % 2
            need(eng, s["lo"], at(B, 1, 1))
            alone(eng)
            if has(B, -2):
                eng.wait_ge(*read_back(nxt(B, -2)))
                alone(eng)
            for qk, dst, runs in ((0, stack_q[r], ((0, 3, 0, 0), (3, 2, 1, 0), (5, 1, 2, 0))),
                                  (1, stack_k[r], ((0, 3, 0, 1), (3, 2, 0, 1), (5, 1, 0, 1)))):
                for c0, n, part, step in runs:
                    src = parts[r][:, part:part + (n if step else 1), qk, :]
                    if not step and n > 1:
                        src = src.to_broadcast([P, n, 256])
                    eng.dma_start(dst[c0:c0 + n, :, :].rearrange("c p t -> p c t"), src).then_inc(written(B)[0], 16)

        def stack_read(eng, B):
            r, r4 = B[1] % 2, B[1] % 4
            eng.wait_ge(*written(B))
            alone(eng)
            need(eng, s["e_ps"], at(B, 6, -18))
            alone(eng)
            for dst, src in ((qs[r4], stack_q[r]), (ks[r4], stack_k[r])):
                for hh in range(2):
                    eng.dma_start(dst[hh * 64:hh * 64 + SPLIT, :, :].rearrange("p g t -> p (g t)"),
                                 src[:, hh * 64:hh * 64 + 64, :].rearrange("c (d g) t -> c d (g t)", g=8)).then_inc(read_back(B)[0], 16)

        @block.sync
        def _(sp):
            for q in range(4):
                sp.dma_start(x_sb[:, 8 * q:8 * q + 8, :],
                             x[8 * q * P:(8 * q + 8) * P, :].rearrange("(t p) d -> p t d", p=P)).then_inc(load_x[q], 16)
                if q == 1:
                    sp.dma_start(cf_sb[:], cf).then_inc(s["load_c"], 16)
                    sp.dma_start(wr_sb[:], wr).then_inc(s["load_c"], 16)
                    sp.dma_start(cb_sb[:], cb).then_inc(s["load_c"], 16)
            sp.wait_ge(s["zeroed"], 1)

            def clear(g):
                sp.dma_start(slot_x[g].rearrange("(p t) d -> p t d", t=NSM[g]), zeros[:, 0:NSM[g], :]).then_inc(slots_clear[g], 16)

            clear(0)
            sp.dma_start(w1_sb[:], w1b.rearrange("e p n -> p e n")).then_inc(s["load_e"], 16)
            sp.dma_start(w2_sb[:], w2.rearrange("e (c p) d -> p e c d", p=P)).then_inc(s["load_e"], 16)
            sp.dma_start(wqk_sb[:, 0, :], wq).then_inc(s["load_w"], 16)
            sp.dma_start(wqk_sb[:, 1, :], wk).then_inc(s["load_w"], 16)
            sp.dma_start(wv_sb[:], wv).then_inc(s["load_w"], 16)
            sp.dma_start(wo_sb[:], wo).then_inc(s["load_w"], 16)
            for r in range(4):
                for hh in range(2):
                    lo = hh * 64 + SPLIT
                    sp.dma_start(qs[r][lo:lo + 6, :, :], qconst[hh]).then_inc(s["load_w"], 16)
                    sp.dma_start(ks[r][lo:lo + 9, :, :], kconst[hh]).then_inc(s["load_w"], 16)

            def experts(f):
                e = fs[f]

                def group(t):
                    return 0 if t < NSG[f][0] else 1

                def load(g, m, c):
                    t = 4 * m + c
                    need(sp, e["xT"], t - 3)
                    if not isinstance(m, int):
                        alone(sp)
                    sp.dma_start(xs[c % 4], slot_x[g][bass.ds((t - NSG[f][0] * g) * P, P), :]).then_inc(e["load"][c % 4], 16)

                def store(g, m, c):
                    t = 4 * m + c
                    sp.wait_ge(e["y"], t + 1)
                    alone(sp)
                    sp.dma_start(slot_y[g][bass.ds((t - NSG[f][0] * g) * P, P), :], ys[c % 4]).then_inc(e["store"][c % 4], 16)

                def one(t):
                    load(group(t), 0, t)
                    store(group(t - 4), 0, t - 4)

                def both(t0, t1):
                    gl, gs = group(t0), group(t0 - 4)
                    rounds = (t1 - t0) // 4
                    with sp.Fori(t0 // 4, t0 // 4 + rounds) as m:
                        for c in range(t0 % 4, t0 % 4 + 4):
                            load(gl, m, c)
                            store(gs, m, c - 4)
                    for t in range(t0 + 4 * rounds, t1):
                        load(gl, 0, t)
                        store(gs, 0, t - 4)

                if f == 1:
                    sp.wait_ge(s["pv_ps"], 2 * (NB - 1))
                sp.wait_ge(e["scattered"][0], 16 * GT[f][0])
                for t in range(4):
                    load(0, 0, t)
                if f == 0:
                    clear(1)
                both(4, NSG[f][0])
                sp.wait_ge(e["scattered"][1], 16 * GT[f][1])
                for t in range(NSG[f][0], NSG[f][0] + 4):
                    load(1, 0, t)
                    store(0, 0, t - 4)
                if f == 1:
                    both(NSG[1][0] + 4, NS)
                else:
                    both(NSG[0][0] + 4, 33)
                    for t in range(33, NS):
                        one(t)
                        if t == 34:
                            stack_write(sp, (0, 0))
                        if t == 36:
                            stack_read(sp, (0, 0))
                for t in range(NS - 4, NS):
                    if f == 0 and t == NS - 4:
                        max_rows((0, 0))
                    store(1, 0, t)

            def max_rows(B):
                r, r4 = B[1] % 2, B[1] % 4
                sp.wait_ge(s["mt_sb"], at(B, 1, 1))
                alone(sp)
                if has(B, -2):
                    sp.wait_ge(max_r[(B[1] - 2) % 4], quarter(nxt(B, -2), 32, 32))
                    alone(sp)
                sp.dma_start(max_d[r], mT[r][:]).then_inc(max_w[r], 16)
                sp.wait_ge(max_w[r], half(B, 16, 16))
                alone(sp)
                need(sp, s["e_ps"], at(B, 6, -18))
                alone(sp)
                for hh in range(2):
                    lo = hh * 64 + KM
                    sp.dma_start(qs[r4][lo:lo + 3, :, :].rearrange("m g t -> m (g t)"),
                                 max_d[r][24 * hh:24 * hh + 24, :].rearrange("(m g) t -> m (g t)", g=8)).then_inc(max_r[r4], 16)

            experts(0)

            def sp_step(B):
                if has(B, 2):
                    stack_write(sp, nxt(B, 2))
                    stack_read(sp, nxt(B, 2))
                if has(B, 1):
                    max_rows(nxt(B, 1))

            steps(sp, sp_step)
            experts(1)

            def store_out(t, n):
                sp.dma_start(out[t * P:(t + n) * P, :].rearrange("(t p) d -> p t d", p=P), x_sb[:, t:t + n, :]).then_inc(fin_o, 16)

            sp.wait_ge(s["fin_x0"], 2)
            store_out(0, T0[1][1] // 2)
            store_out(T0[1][1] // 2, T0[1][1] // 2)
            for k in range(GT[1][1] // 4):
                sp.wait_ge(s["fin_x"], k + 1)
                store_out(T0[1][1] + 4 * k, 4)
            sp.wait_ge(fin_o, 16 * (2 + GT[1][1] // 4))

        @block.gpsimd
        def _(pool):
            nc.gpsimd.memset(zeros, 0.0).then_inc(s["zeroed"], 1)
            for r in range(2):
                nc.gpsimd.memset(vaug[r][:], 1.0).then_inc(s["attn_vones"], 1)

            def scatter(f, g, t0, t1):
                if t0 == T0[f][g]:
                    pool.wait_ge(s["place"], 2 * f + g + 1)
                    if f == 0:
                        pool.wait_ge(slots_clear[g], 16)
                if f == 1:
                    pool.wait_ge(s["r_copied"], (t1 + 1) // 2)
                for t in range(t0, t1):
                    nc.gpsimd.indirect_dma_start(
                        out=slot_x[g][0:NSG[f][g] * P, :], out_offset=bass.IndirectOffsetOnAxis(ap=slot_i[:, t:t + 1], axis=0),
                        in_=xh_all[:, t, :], in_offset=None).then_inc(fs[f]["scattered"][g], 16)

            def stored(f, g):
                for r in range(4):
                    pool.wait_ge(fs[f]["store"][r], 16 * len(range(r, NS if g else NSG[f][0], 4)))

            def gather(f, t, semaphore):
                g = 0 if t < GT[f][0] else 1
                nc.gpsimd.indirect_dma_start(
                    out=xh_all[:, t, :], out_offset=None,
                    in_=slot_y[g][0:NSG[f][g] * P, :], in_offset=bass.IndirectOffsetOnAxis(ap=slot_i[:, t:t + 1], axis=0)).then_inc(semaphore, 16)

            pool.wait_ge(s["load_c"], 48)
            for g in range(2):
                t0, t1 = T0[0][g], T0[0][g] + GT[0][g]
                pool.wait_ge(s["lnst"], g + 1)
                nc.gpsimd.tensor_tensor(rstd_all[:, t0:t1], ln_c[:, t0:t1], minus_half[:, t0:t1], ALU.pow).then_inc(s["lnpow"], 1)
            scatter(0, 0, 0, GT[0][0])
            scatter(0, 1, GT[0][0], NT)
            stored(0, 0)
            for t in range(GT[0][0]):
                gather(0, t, got_y[0 if t < ROWS_SOON else 5])

            def power(B):
                r = B[1] % 2
                pool.wait_ge(s["aggr"], at(B, 1, 1))
                alone(pool)
                nc.gpsimd.tensor_scalar(veps[r][:], mv[r][:, :, 1], EPS, None, ALU.add).then_inc(s["veps"], 1)
                pool.wait_ge(s["veps"], at(B, 1, 1))
                need(pool, s["ln_xh"], at(B, 1, -1))
                nc.gpsimd.tensor_tensor(rstd[r][:], veps[r][:], minus_half[:, 0:2], ALU.pow).then_inc(s["ln_pow"], 1)

            def low(B):
                r = B[1] % 2
                pool.wait_ge(s["mid"], at(B, 1, 1))
                nc.gpsimd.tensor_tensor(parts[r][:, 2, :, :], rest[:].rearrange("p (a t) -> p a t", a=2),
                                        parts[r][:, 1, :, :], ALU.subtract).then_inc(s["lo"], 1)

            def r_power(B):
                r = B[1] % 2
                pool.wait_ge(s["r_aggr"], at(B, 1, 1))
                alone(pool)
                nc.gpsimd.tensor_scalar(veps3[r][:], mv3[r][:, :, 1], EPS, None, ALU.add).then_inc(s["r_veps"], 1)
                pool.wait_ge(s["r_veps"], at(B, 1, 1))
                need(pool, s["r_xh"], at(B, 1, -1))
                nc.gpsimd.tensor_tensor(rstd3[r][:], veps3[r][:], minus_half[:, 0:2], ALU.pow).then_inc(s["r_pow"], 1)

            for b in range(3):
                power((0, b))
            low((0, 0))
            low((0, 1))
            stack_write(pool, (0, 1))
            stack_read(pool, (0, 1))

            def pool_step(B):
                if is_step(B, 0):
                    stored(0, 1)
                if isinstance(B[0], int) and B[1] < 4:
                    for t in range(GT[0][0] + ROWS * B[1], GT[0][0] + ROWS * (B[1] + 1)):
                        gather(0, t, got_y[1 + B[1]])
                if has(B, 2):
                    low(nxt(B, 2))
                if has(B, 3):
                    power(nxt(B, 3))
                if has(B, -2):
                    r_power(nxt(B, -2))
                if is_step(B, 13):
                    scatter(1, 0, 0, GT[1][0] // 2)
                if is_step(B, 14):
                    scatter(1, 0, GT[1][0] // 2, GT[1][0])

            steps(pool, pool_step)
            for b in (NB - 2, NB - 1):
                r_power((0, b))
            scatter(1, 1, GT[1][0], NT)
            stored(1, 0)
            n = GT[1][0]
            for t in range(n):
                gather(1, t, fin_y[4])
            pool.wait_ge(fin_y[4], 16 * n)
            nc.gpsimd.tensor_tensor(xh_all[:, 0:n, :], xh_all[:, 0:n, :],
                                    pmax[:, 0:n].rearrange("p (t o) -> p t o", o=1).to_broadcast([P, n, D]), ALU.mult).then_inc(s["fin_x0"], 1)
            pool.wait_ge(s["fin_x0"], 1)
            nc.gpsimd.tensor_tensor(x_sb[:, 0:n, :], xh_all[:, 0:n, :], x_sb[:, 0:n, :], ALU.add).then_inc(s["fin_x0"], 1)
            stored(1, 1)
            for t in range(n, NT):
                gather(1, t, fin_y[(t - n) // 4])

        @block.scalar
        def _(act):
            def copies(g):
                for n in range(T0[0][g] // 4, (T0[0][g] + GT[0][g]) // 4):
                    act.wait_ge(s["tr"], n + 1)
                    need(act, s["lg"], n - 1)
                    nc.scalar.activation(xhT[n % 2], (pA, pB)[n % 2][:], ACT.Copy).then_inc(s["trc"], 1)

            def exp_logits(n):
                act.wait_ge(s["diff"], n + 1)
                w = GT[n // 2][n % 2]
                nc.scalar.activation(lexp[:, 0:w, :], cand[:, 0:w, :], ACT.Exp).then_inc(s["lexp"], 1)

            def experts(f):
                e = fs[f]

                def gelu(m, c):
                    t = 4 * m + c
                    act.wait_ge(e["up"], t + 1)
                    need(act, e["down"], t - 1)
                    for k in range(FC):
                        i = nc.scalar.activation(hT[c % 2][:, k, :], pE[:, (c % 2) * 512 + k * P:(c % 2) * 512 + (k + 1) * P],
                                                 ACT.Gelu, bias=w1_st[c % 4][:, F + k:F + k + 1])
                    i.then_inc(e["gelu"], 1)

                def tiles_between(t0, t1):
                    with act.Fori(t0 // 4, t1 // 4) as m:
                        for c in range(4):
                            gelu(m, c)
                return gelu, tiles_between

            for g in range(2):
                copies(g)
                exp_logits(g)

            def copy_x(B, bank=pB):
                act.wait_ge(s["xt_ps"], at(B, 1, 1))
                need(act, s["v_ps"], at(B, 1, -3))
                nc.scalar.activation(xT[B[1] % 4][:], bank[:, 0:256], ACT.Copy).then_inc(s["xt_sb"], 1)

            def high(B):
                r = B[1] % 2
                act.wait_ge(s["qk_ps"], at(B, 1, 1))
                if has(B, -2):
                    act.wait_ge(*written(nxt(B, -2)))
                nc.scalar.activation(parts[r][:, 0, :, :], pA[:].rearrange("p (a t) -> p a t", a=2), ACT.Copy,
                                     scale=QK_SCALE).then_inc(s["hi"], 1)

            def second(B):
                act.wait_ge(s["rest"], at(B, 1, 1))
                nc.scalar.activation(parts[B[1] % 2][:, 1, :, :], rest[:].rearrange("p (a t) -> p a t", a=2), ACT.Copy).then_inc(s["mid"], 1)

            def copy_v(B):
                r = B[1] % 2
                act.wait_ge(s["v_ps"], at(B, 1, 1))
                need(act, s["pv_ps"], at(B, 2, -2))
                nc.scalar.activation(vaug[r][:, :, :, 0:HD], pB[:, 256:512].rearrange("p (a h d) -> p a h d", a=2, d=HD), ACT.Copy).then_inc(s["v_sb"], 1)

            def copy_m(B, source=pMT):
                act.wait_ge(s["mt_ps"], at(B, 1, 1))
                need(act, max_w[B[1] % 2], half(B, 16))
                nc.scalar.activation(mT[B[1] % 2][:], source, ACT.Copy).then_inc(s["mt_sb"], 1)

            def exps(B, u):
                r = B[1] % 2
                act.wait_ge(s["e_ps"], at(B, 6, u + 1))
                if u == 0:
                    need(act, s["pv_ps"], at(B, 2, -2))
                if is_step(B, 0) and u == 0:
                    act.wait_ge(fs[0]["y"], NS)
                if is_step(B, 0) and u == 4:
                    for r4 in range(4):
                        act.wait_ge(fs[0]["store"][r4], 16 * len(range(r4, NS, 4)))
                dst = pt0[r][:, u, :, :, :] if u < 4 else pt1[r][:, u - 4, :, :, :]
                w = 256 if u < 4 else 128
                nc.scalar.activation(dst, score_banks(B, u).rearrange("p (a b t) -> p a b t", a=2, t=w), ACT.Exp).then_inc(s["e_sb"], 1)

            def copy_pv(B, k):
                act.wait_ge(s["pv_ps"], at(B, 2, k + 1))
                need(act, s["back_ps"], at(B, 2, k - 1))
                nc.scalar.activation(outT[k][:], pO[:], ACT.Copy).then_inc(s["pv_sb"], 1)

            def copy_o(B):
                act.wait_ge(s["ot_ps"], at(B, 1, 1))
                need(act, s["wo_ps"], at(B, 1, -1))
                nc.scalar.activation(oT[B[1] % 2][:], pC[:, 0:256], ACT.Copy).then_inc(s["ot_sb"], 1)

            gelu, tiles_between = experts(0)
            for t in range(4):
                gelu(0, t)
            tiles_between(4, EARLY)
            b0, b1 = (0, 0), (0, 1)
            for t in range(EARLY, NS):
                gelu(0, t)
                if t == 28:
                    copy_x(b0, pC)
                if t == 29:
                    high(b0)
                    copy_x(b1, pC)
                if t == 30:
                    second(b0)
                if t == 31:
                    high(b1)
                if t == 32:
                    second(b1)
                if t == 43:
                    copy_m(b0, pMT_early)

            def r_keep(B):
                act.wait_ge(s["r_xh"], at(B, 1, 1))
                nc.scalar.activation(xh_all[:, tiles(B), :], xr[B[1] % 2][:], ACT.Copy).then_inc(s["r_copied"], 1)

            def r_copy(B):
                act.wait_ge(s["r_tps"], at(B, 1, 1))
                need(act, s["r_lps"], at(B, 1))
                nc.scalar.activation(xrT[:], pA[:, 0:256], ACT.Copy).then_inc(s["r_tsb"], 1)

            def act_step(B):
                if is_step(B, 14):
                    exp_logits(2)
                if has(B, 2):
                    copy_x(nxt(B, 2))
                    high(nxt(B, 2))
                if has(B, -3):
                    r_keep(nxt(B, -3))
                if has(B, 0):
                    exps(B, 0)
                if has(B, 2):
                    second(nxt(B, 2))
                if has(B, -2):
                    copy_o(nxt(B, -2))
                if has(B, 0):
                    exps(B, 1)
                    exps(B, 2)
                    copy_v(B)
                    exps(B, 3)
                    exps(B, 4)
                if has(B, -1):
                    copy_pv(nxt(B, -1), 0)
                if has(B, 1):
                    copy_m(nxt(B, 1))
                if has(B, 0):
                    exps(B, 5)
                if has(B, -3):
                    r_copy(nxt(B, -3))
                if has(B, -1):
                    copy_pv(nxt(B, -1), 1)

            act.wait_ge(s["attn_vones"], 2)
            steps(act, act_step)
            gelu, tiles_between = experts(1)
            b14, b15 = (0, NB - 2), (0, NB - 1)
            copy_o(b14)
            gelu(0, 0)
            copy_pv(b15, 0)
            gelu(0, 1)
            r_keep((0, NB - 3))
            gelu(0, 2)
            r_copy((0, NB - 3))
            copy_pv(b15, 1)
            gelu(0, 3)
            gelu(0, 4)
            r_keep(b14)
            copy_o(b15)
            gelu(0, 5)
            r_copy(b14)
            gelu(0, 6)
            gelu(0, 7)
            r_keep(b15)
            r_copy(b15)
            gelu(0, 8)
            exp_logits(3)
            for t in range(9, 12):
                gelu(0, t)
            tiles_between(12, 44)
            for t in range(44, NS):
                gelu(0, t)

        @block.tensor
        def _(pe):
            pe.wait_ge(s["load_c"], 48)

            def logits(g):
                def turn(n):
                    pe.wait_ge(s["xh"], n + 1)
                    need(pe, s["trc"], n - 1)
                    for j in range(4):
                        i = pe.transpose((pA, pB)[n % 2][:, j * P:(j + 1) * P], xh_all[:, 4 * n + j, :], ident_f)
                    i.then_inc(s["tr"], 1)

                n0, n1 = T0[0][g] // 4, (T0[0][g] + GT[0][g]) // 4
                turn(n0)
                for n in range(n0, n1):
                    if n < n1 - 1:
                        turn(n + 1)
                    pe.wait_ge(s["trc"], n + 1)
                    for j in range(4):
                        i = pe.matmul(pM[0][:, (4 * n + j) * NE:(4 * n + j + 1) * NE], xhT[n % 2][:, j * P:(j + 1) * P], wr_sb[:],
                                      start=True, stop=True)
                    i.then_inc(s["lg"], 1)

            def ranks(n, bank):
                pe.wait_ge(s["route"], n + 1)
                w = NE * GT[n // 2][n % 2]
                oh = onehot[:, 0:w]
                pe.matmul(bank[:, 0:w], before, oh, start=True, stop=True)
                pe.matmul(bank[:, 256:256 + w], ones_b, oh, start=True, stop=True).then_inc(s["rank"], 1)

            def experts(f):
                e = fs[f]

                def turn(m, c):
                    t = 4 * m + c
                    pe.wait_ge(e["load"][c % 4], 16 * m + 16 * (c // 4 + 1))
                    need(pe, e["xTc"], t)
                    pe.transpose(pB[:, 0:P], xs[c % 4], ident_f).then_inc(e["xT"], 1)

                def up(m, c):
                    t = 4 * m + c
                    pe.wait_ge(e["w1c"], t + 1)
                    pe.wait_ge(e["xTc"], t + 1)
                    need(pe, e["gelu"], t - 1)
                    for k in range(FC):
                        i = pe.matmul(pE[:, (c % 2) * 512 + k * P:(c % 2) * 512 + (k + 1) * P],
                                      w1_st[c % 4][:, k * P:(k + 1) * P], xsT[c % 2], start=True, stop=True)
                    i.then_inc(e["up"], 1)

                def expert(m, c):
                    t = 4 * m + c
                    return pe.value_load(expert_i[0:1, bass.ds(t, 1)], min_val=0, max_val=NE - 1)

                def down(m, c, x):
                    t = 4 * m + c
                    pe.wait_ge(e["gelu"], t + 1)
                    need(pe, e["y"], t - 1)
                    for k in range(FC):
                        i = pe.matmul(pM[c % 2][:, 0:D], hT[c % 2][:, k, :],
                                      w2_sb[:, bass.ds(x, 1), k, :].rearrange("p o d -> p (o d)"), start=(k == 0), stop=(k == FC - 1))
                    i.then_inc(e["down"], 1)

                def start():
                    pe.wait_ge(s["ts"], 2 * f + 1)
                    turn(0, 0)
                    turn(0, 1)
                    if f == 0:
                        ranks(1, pA)
                    up(0, 0)

                def tile(m, c):
                    if not isinstance(m, int) or c + 1 < NS:
                        turn(m, c + 1)
                    up(m, c)
                    down(m, c - 1, expert(m, c - 1))

                def tiles_between(t0, t1):
                    with pe.Fori(t0 // 4, t1 // 4) as m:
                        for c in range(4):
                            tile(m, c)

                def end():
                    down(0, NS - 1, expert(0, NS - 1))
                return start, tile, tiles_between, end

            logits(0)
            ranks(0, pA)
            logits(1)
            pe.wait_ge(s["load_e"], 32)

            def turn_x(B, bank=pB):
                r = B[1] % 2
                pe.wait_ge(s["ln_xh"], at(B, 1, 1))
                if has(B, -2):
                    pe.wait_ge(s["mt_sb"], at(B, 1, -1))
                else:
                    need(pe, s["xt_sb"], at(B, 1))
                for j in range(2):
                    i = pe.transpose(bank[:, j * P:(j + 1) * P], xh[r][:, j, :], ident_f)
                i.then_inc(s["xt_ps"], 1)

            def project_qk(B):
                pe.wait_ge(s["xt_sb"], at(B, 1, 1))
                need(pe, s["rest"], at(B, 1))
                if has(B, -5):
                    need(pe, s["r_lg"], at(B, 1, -5))
                for a in range(2):
                    i = pe.matmul(pA[:, a * 256:(a + 1) * 256], wqk_sb[:, a, :], xT[B[1] % 4][:], start=True, stop=True)
                i.then_inc(s["qk_ps"], 1)

            def project_v(B):
                if has(B, 2):
                    pe.wait_ge(s["xt_sb"], at(B, 1, 3))
                else:
                    pe.wait_ge(s["mt_sb"], at(B, 1, 1))
                for j in range(2):
                    i = pe.matmul(pB[:, 256 + j * P:256 + (j + 1) * P], xT[B[1] % 4][:, j * P:(j + 1) * P], wv_sb[:], start=True, stop=True)
                i.then_inc(s["v_ps"], 1)

            def maxima(B, u, banks=pM):
                r = B[1] % 4
                if u == 0:
                    pe.wait_ge(*read_back(B))
                if u < 4:
                    n, w, g0 = 2, 256, 2 * u
                else:
                    n, w, g0 = 4, 128, 4 * (u - 4)
                if is_step(B, NB - 1) and u == 0:
                    pe.wait_ge(s["ranks_sb"], 3)
                if is_step(B, 1) and u == 0:
                    pe.wait_ge(fs[0]["y"], NS)
                v = [bank.rearrange("p (n w) -> p n w", w=w) for bank in banks]
                q0 = 128 if u < 4 else 0
                for hh in range(2):
                    need(pe, s["m_neg"], at(B, 12, 2 * u + hh - 1))
                    pe.matmul(v[hh][:, :, w - 128:w], ident_b, mask_q.rearrange("p (o k) -> p o k", o=1).to_broadcast([P, n, P]),
                              start=True, stop=False, skip_group_check=True)
                for j in range(n):
                    for hh in range(2):
                        i = pe.matmul(v[hh][:, j, :], qs[r][hh * 64:hh * 64 + KM, g0 + j, q0:q0 + 128],
                                      ks[r][hh * 64:hh * 64 + KM, g0 + j, 0:w], start=False, stop=(j == n - 1), skip_group_check=True)
                        if j == n - 1:
                            i.then_inc(s["m_ps"], 1)

            def scores(B, u):
                r = B[1] % 4
                if u == 0:
                    pe.wait_ge(max_r[r], quarter(B, 32, 32))
                if is_step(B, NB - 1):
                    need(pe, s["e_sb"], at(B, 6, u - 1 + (u == 0)))
                    pe.wait_ge(s["m_neg"], 12 * NB)
                else:
                    need(pe, s["e_sb"], at(B, 6, u))
                if u < 4:
                    n, w, g0, k0 = 2, 256, 2 * u, 0
                else:
                    n, w, g0, k0 = 4, 128, 4 * (u - 4), 128
                v = score_banks(B, u).rearrange("p (a n w) -> p a n w", a=2, w=w)
                for hh in range(2):
                    pe.matmul(v[:, hh, :, 0:128], ident_b, mask_k.rearrange("p (o k) -> p o k", o=1).to_broadcast([P, n, P]),
                              start=True, stop=False, skip_group_check=True)
                for j in range(n):
                    for hh in range(2):
                        i = pe.matmul(v[:, hh, j, :], ks[r][hh * 64:hh * 64 + KE, g0 + j, k0:k0 + 128],
                                      qs[r][hh * 64:hh * 64 + KE, g0 + j, 256 - w:256], start=False, stop=(j == n - 1), skip_group_check=True)
                i.then_inc(s["e_ps"], 1)

            def attend(B, u):
                r = B[1] % 2
                if u == 0:
                    pe.wait_ge(s["e_sb"], at(B, 6, 6))
                    pe.wait_ge(s["v_sb"], at(B, 1, 1))
                if u % 2 == 0:
                    need(pe, s["pv_sb"], at(B, 2, u // 2))
                for keys in range(2):
                    for j in range(4):
                        o = pO[32 * j:32 * j + VW, (u % 2) * 256 + keys * 128:(u % 2) * 256 + 256]
                        p = pt0[r][:, u, j % 2, j // 2, :] if keys == 0 else pt1[r][:, u // 2, j % 2, 2 * (u % 2) + j // 2, :]
                        i = pe.matmul(o, vaug[r][:, keys, 4 * u + j, :], p, start=(keys == 0), stop=(keys == 1), skip_group_check=True)
                if u % 2:
                    i.then_inc(s["pv_ps"], 1)

            def turn_back(B, k):
                pe.wait_ge(s["pv_sb"], at(B, 2, k + 1))
                if k == 0:
                    need(pe, s["x_attn"], at(B, 1))
                else:
                    pe.wait_ge(s["o_nrm"], at(B, 2, 1))
                for j in range(2):
                    for a in range(2):
                        i = pe.transpose(pC[:, j * 256 + a * P:j * 256 + (a + 1) * P], outT[k][:, a * 256 + j * P:a * 256 + (j + 1) * P], ident_f)
                i.then_inc(s["back_ps"], 1)

            def turn_m(B, target=pMT):
                r = B[1] % 2
                pe.wait_ge(s["m_split"], at(B, 1, 1))
                if has(B, -1):
                    pe.wait_ge(s["v_sb"], at(B, 1))
                alone(pe)
                for j in range(2):
                    i = pe.transpose(target[:, j * P:(j + 1) * P], mparts[r][:, j, :, :, :].rearrange("p a m g -> p (a m g)"), ident_b)
                i.then_inc(s["mt_ps"], 1)

            def turn_o(B):
                r = B[1] % 2
                pe.wait_ge(s["o_nrm"], at(B, 2, 2))
                for j in range(2):
                    i = pe.transpose(pC[:, j * P:(j + 1) * P], o_sb[r][:, j, :], ident_f)
                i.then_inc(s["ot_ps"], 1)

            def project_o(B):
                r = B[1] % 2
                pe.wait_ge(s["ot_sb"], at(B, 1, 1))
                for j in range(2):
                    i = pe.matmul(pC[:, 256 + j * P:256 + (j + 1) * P], oT[r][:, j * P:(j + 1) * P], wo_sb[:], start=True, stop=True)
                i.then_inc(s["wo_ps"], 1)

            def r_turn(B):
                pe.wait_ge(s["r_xh"], at(B, 1, 1))
                if has(B, 5):
                    pe.wait_ge(s["rest"], at(B, 1, 6))
                else:
                    pe.wait_ge(s["rest"], NB)
                    pe.wait_ge(s["r_lg"], at(B, 1))
                for j in range(2):
                    i = pe.transpose(pA[:, j * P:(j + 1) * P], xr[B[1] % 2][:, j, :], ident_f)
                i.then_inc(s["r_tps"], 1)

            def r_logits(B):
                pe.wait_ge(s["r_tsb"], at(B, 1, 1))
                for j in range(2):
                    i = pe.matmul(pA[:, 256 + j * NE:256 + (j + 1) * NE], xrT[:, j * P:(j + 1) * P], wr_sb[:], start=True, stop=True)
                i.then_inc(s["r_lps"], 1)

            start, tile, tiles_between, end = experts(0)
            start()
            for t in range(1, 4):
                tile(0, t)
            tiles_between(4, EARLY)
            b0, b1 = (0, 0), (0, 1)
            pe.wait_ge(s["load_w"], LOADED)
            for t in range(EARLY, NS):
                tile(0, t)
                if t == 28:
                    turn_x(b0, pC)
                if t == 29:
                    project_qk(b0)
                    turn_x(b1, pC)
                if t == 31:
                    project_qk(b1)
                if 36 <= t < 42:
                    maxima(b0, t - 36, (pO[:], pC[:]))
                if t == 43:
                    turn_m(b0, pMT_early)
            end()

            def pe_step(B):
                if has(B, 2):
                    turn_x(nxt(B, 2))
                if has(B, 1):
                    maxima(nxt(B, 1), 0)
                if has(B, -2):
                    turn_back(nxt(B, -2), 1)
                if has(B, 2):
                    project_qk(nxt(B, 2))
                if has(B, 1):
                    maxima(nxt(B, 1), 1)
                if has(B, 0):
                    scores(B, 0)
                if has(B, 1):
                    maxima(nxt(B, 1), 2)
                if has(B, -2):
                    turn_o(nxt(B, -2))
                if has(B, 0):
                    scores(B, 1)
                if has(B, -1):
                    attend(nxt(B, -1), 0)
                if has(B, 1):
                    maxima(nxt(B, 1), 3)
                if has(B, -2):
                    project_o(nxt(B, -2))
                if has(B, 0):
                    scores(B, 2)
                if has(B, 1):
                    maxima(nxt(B, 1), 4)
                if has(B, 0):
                    project_v(B)
                    scores(B, 3)
                if has(B, 1):
                    maxima(nxt(B, 1), 5)
                if has(B, 0):
                    scores(B, 4)
                if has(B, -1):
                    attend(nxt(B, -1), 1)
                if has(B, 1):
                    turn_m(nxt(B, 1))
                if has(B, 0):
                    scores(B, 5)
                if has(B, -3):
                    r_turn(nxt(B, -3))
                if has(B, -1):
                    turn_back(nxt(B, -1), 0)
                    attend(nxt(B, -1), 2)
                if has(B, -3):
                    r_logits(nxt(B, -3))
                if is_step(B, 13):
                    pe.wait_ge(s["m_neg"], at(B, 12, 24))
                    ranks(2, pM[0])
                if has(B, -1):
                    attend(nxt(B, -1), 3)

            steps(pe, pe_step)
            start, tile, tiles_between, end = experts(1)
            b14, b15 = (0, NB - 2), (0, NB - 1)
            turn_back(b14, 1)
            attend(b15, 0)
            turn_o(b14)
            start()
            attend(b15, 1)
            tile(0, 1)
            project_o(b14)
            turn_back(b15, 0)
            tile(0, 2)
            r_turn((0, NB - 3))
            attend(b15, 2)
            r_logits((0, NB - 3))
            attend(b15, 3)
            tile(0, 3)
            turn_back(b15, 1)
            tile(0, 4)
            turn_o(b15)
            tile(0, 5)
            project_o(b15)
            r_turn(b14)
            tile(0, 6)
            r_logits(b14)
            tile(0, 7)
            r_turn(b15)
            tile(0, 8)
            r_logits(b15)
            tile(0, 9)
            pe.wait_ge(s["r_lg"], NB)
            ranks(3, pA)
            tile(0, 10)
            tile(0, 11)
            tiles_between(12, 44)
            for t in range(44, NS):
                tile(0, t)
            end()

        @block.vector
        def _(dve):
            V = nc.vector

            link = [0]

            def then(ins):
                link[0] += 1
                ins.then_inc(s["chain"], 1)
                dve.wait_ge(s["chain"], link[0])

            def moments(g):
                t0, n = T0[0][g], GT[0][g]
                t1 = t0 + n
                for t in range(t0, t1):
                    if t % 8 == 0:
                        dve.wait_ge(load_x[t // 8], 16)
                    i = V.bn_stats(st_all[:, t, :], x_sb[:, t, :])
                then(i)
                me, mo, ve, vo = (st_all[:, t0:t1, k] for k in (1, 4, 2, 5))
                a, b = ln_a[:, 0:n], ln_b[:, 0:n]
                V.tensor_tensor(mean_all[:, t0:t1], me, mo, ALU.add)
                V.tensor_tensor(a, me, mo, ALU.subtract)
                then(V.tensor_tensor(b, ve, vo, ALU.add))
                then(V.scalar_tensor_tensor(ln_c[:, t0:t1], a, 0.25, a, ALU.mult, ALU.mult))
                then(V.scalar_tensor_tensor(a, b, 1.0 / D, ln_c[:, t0:t1], ALU.mult, ALU.add))
                V.tensor_scalar(ln_c[:, t0:t1], a, EPS, None, ALU.add).then_inc(s["lnst"], 1)
                then(V.tensor_scalar(mean_all[:, t0:t1], mean_all[:, t0:t1], 0.5, None, ALU.mult))

            def normed(g):
                dve.wait_ge(s["lnpow"], g + 1)
                for t in range(T0[0][g], T0[0][g] + GT[0][g]):
                    i = V.tensor_scalar(xh_all[:, t, :], x_sb[:, t, :], mean_all[:, t:t + 1], rstd_all[:, t:t + 1],
                                        ALU.subtract, ALU.mult)
                    if t % 4 == 3:
                        i.then_inc(s["xh"], 1)

            def choose(n):
                f, g = n // 2, n % 2
                t0, w = T0[f][g], GT[f][g]
                lg, eq, lm, ch = lg_all[:, t0:t0 + w, :], equal[:, 0:w, :], lmax[:, 0:w], chosen[:, 0:w]
                if f == 0:
                    dve.wait_ge(s["lg"], (t0 + w) // 4)
                    then(V.tensor_copy(lg, pM[0][:, NE * t0:NE * (t0 + w)].rearrange("p (t e) -> p t e", e=NE)))
                else:
                    dve.wait_ge(s["r_lg"], (t0 + w) // 2)
                then(V.tensor_reduce(lm, lg, AX.X, ALU.max))
                V.tensor_tensor(cand[:, 0:w, :], lg, lm.rearrange("p (t o) -> p t o", o=1).to_broadcast([P, w, NE]),
                                ALU.subtract).then_inc(s["diff"], 1)
                dve.wait_ge(s["diff"], n + 1)
                then(V.tensor_scalar(eq, cand[:, 0:w, :], 0.0, None, ALU.is_equal))
                then(V.tensor_tensor(eq, eq, rank8.rearrange("p (o e) -> p o e", o=1).to_broadcast([P, w, NE]), ALU.mult))
                then(V.tensor_reduce(ch, eq, AX.X, ALU.max))
                V.tensor_tensor(onehot[:, 0:NE * w].rearrange("p (e t) -> p e t", e=NE), rank8.rearrange("p (e o) -> p e o", o=1).to_broadcast([P, NE, w]),
                                ch.rearrange("p (o t) -> p o t", o=1).to_broadcast([P, NE, w]), ALU.is_equal).then_inc(s["route"], 1)

            def half_probability(n):
                f, g = n // 2, n % 2
                t0, w = T0[f][g], GT[f][g]
                lm = lmax[:, 0:w]
                dve.wait_ge(s["lexp"], n + 1)
                then(V.tensor_reduce(lm, lexp[:, 0:w, :], AX.X, ALU.add))
                then(V.reciprocal(lm, lm))
                then(V.tensor_scalar(pmax[:, t0:t0 + w], lm, 0.5, None, ALU.mult))

            def places(n, bank):
                f, g = n // 2, n % 2
                w = GT[f][g]
                dve.wait_ge(s["rank"], n + 1)
                rank = bank[:, 0:NE * w].rearrange("p (e t) -> p e t", e=NE)
                total = bank[:, 256:256 + NE * w].rearrange("p (e t) -> p e t", e=NE)
                fi, up, pl, oh = (a[:, 0:NE * w].rearrange("p (e t) -> p e t", e=NE) for a in (fills, upto, place, onehot))
                V.tensor_copy(pl, rank)
                V.tensor_copy(fi, total).then_inc(s["ranks_sb"], 1)
                dve.wait_ge(s["ranks_sb"], n + 1)
                then(V.tensor_tensor_scan(upto[:, 0:NE * w], keep[n], fills[:, 0:NE * w], 0.0, ALU.mult, ALU.add))
                then(V.tensor_tensor(pl, pl, up, ALU.add))
                then(V.tensor_tensor(pl, pl, fi, ALU.subtract))
                then(V.tensor_tensor(fi, up[:, :, w - 1:w].to_broadcast([P, NE, w]),
                                     steps128[:, 0:w].rearrange("p (o t) -> p o t", o=1).to_broadcast([P, NE, w]), ALU.is_gt))
                then(V.tensor_reduce(ntiles[:], fi, AX.X, ALU.add))
                then(V.tensor_tensor_scan(tile_end[:], ones8, ntiles[:], 0.0, ALU.mult, ALU.add))
                then(V.tensor_tensor(tile_start[:], tile_end[:], ntiles[:], ALU.subtract))
                then(V.tensor_scalar(tile_start[:], tile_start[:], float(P), None, ALU.mult))
                then(V.tensor_tensor(pl, pl, tile_start[:].rearrange("p (e o) -> p e o", o=1).to_broadcast([P, NE, w]), ALU.add))
                then(V.tensor_tensor(pl, pl, oh, ALU.mult))
                then(V.tensor_reduce(slot_f[:, 0:w], pl.rearrange("p e t -> p t e"), AX.X, ALU.add))
                V.tensor_copy(slot_i[:, T0[f][g]:T0[f][g] + w], slot_f[:, 0:w]).then_inc(s["place"], 1)

            def experts_of(n):
                f, g = n // 2, n % 2
                slots = NSG[f][g]
                ec = expert_cmp[:, 0:slots, :]
                then(V.tensor_tensor(ec, slot_ids[:, 0:slots].rearrange("p (s o) -> p s o", o=1).to_broadcast([P, slots, NE - 1]),
                                     tile_end[:, 0:NE - 1].rearrange("p (o e) -> p o e", o=1).to_broadcast([P, slots, NE - 1]), ALU.is_ge))
                then(V.tensor_reduce(expert_f[:, 0:slots], ec, AX.X, ALU.add))
                i0 = NSG[f][0] * g
                V.tensor_copy(expert_i[:, i0:i0 + slots], expert_f[:, 0:slots]).then_inc(s["ts"], 1)

            def experts(f):
                e = fs[f]

                def copy_w1(m, c):
                    t = 4 * m + c
                    x = dve.value_load(expert_i[0:1, bass.ds(t, 1)], min_val=0, max_val=NE - 1)
                    need(dve, e["gelu"], t - 3)
                    need(dve, e["y"], t - 3)
                    V.tensor_copy(w1_st[c % 4], w1_sb[:, bass.ds(x, 1), :].rearrange("p o n -> p (o n)")).then_inc(e["w1c"], 1)

                def copy_x(m, c):
                    t = 4 * m + c
                    dve.wait_ge(e["xT"], t + 1)
                    need(dve, e["up"], t - 1)
                    V.tensor_copy(xsT[c % 2], pB[:, 0:P]).then_inc(e["xTc"], 1)

                def add_bias(m, c):
                    t = 4 * m + c
                    if not isinstance(m, int) or c >= 4:
                        dve.wait_ge(e["store"][c % 4], 16 * m + 16 * (c // 4))
                    dve.wait_ge(e["down"], t + 1)
                    V.tensor_tensor(ys[c % 4], pM[c % 2][:, 0:D], w1_st[c % 4][:, F + FC:W1W], ALU.add).then_inc(e["y"], 1)

                def start():
                    if f == 1:
                        dve.wait_ge(s["pv_ps"], 2 * (NB - 1))
                    dve.wait_ge(s["ts"], 2 * f + 1)
                    for c in range(3):
                        copy_w1(0, c)
                    if f == 0:
                        choose(1)
                    copy_x(0, 0)
                    copy_x(0, 1)
                    if f == 0:
                        places(1, pA)
                        experts_of(1)

                def tile(m, c):
                    if not isinstance(m, int) or c + 2 < NS:
                        copy_x(m, c + 2)
                    if not isinstance(m, int) or c + 3 < NS:
                        copy_w1(m, c + 3)
                    add_bias(m, c)

                def tiles_between(t0, t1):
                    with dve.Fori(t0 // 4, t1 // 4) as m:
                        for c in range(4):
                            tile(m, c)
                return start, tile, tiles_between

            moments(0)
            normed(0)
            moments(1)
            dve.wait_ge(s["load_c"], 48)
            choose(0)
            places(0, pA)
            experts_of(0)
            normed(1)
            half_probability(0)
            dve.wait_ge(s["load_e"], 32)

            def residual(B):
                r = B[1] % 2
                if is_step(B, 0):
                    dve.wait_ge(got_y[0], 16 * ROWS_SOON)
                if is_step(B, 3):
                    dve.wait_ge(got_y[5], 16 * (GT[0][0] - ROWS_SOON))
                if is_step(B, 6):
                    dve.wait_ge(got_y[1], 16 * ROWS)
                if not isinstance(B[0], int) and B[1] == 3:
                    for k in (2, 3, 4):
                        dve.wait_ge(got_y[k], 16 * ROWS)
                for j in range(2):
                    t = at(B, 2, j)
                    xt = x_sb[:, bass.ds(t, 1), :].rearrange("p o d -> p (o d)")
                    i = V.scalar_tensor_tensor(xt, xh_all[:, bass.ds(t, 1), :].rearrange("p o d -> p (o d)"), pmax[:, bass.ds(t, 1)], xt, ALU.mult, ALU.add)
                i.then_inc(s["res_x"], 1)
                dve.wait_ge(s["res_x"], at(B, 1, 1))
                alone(dve)
                for j in range(2):
                    t = at(B, 2, j)
                    i = V.bn_stats(st2[r][:, j, :], x_sb[:, bass.ds(t, 1), :].rearrange("p o d -> p (o d)"))
                i.then_inc(s["stats"], 1)
                dve.wait_ge(s["stats"], at(B, 1, 1))
                need(dve, s["veps"], at(B, 1, -1))
                alone(dve)
                for j in range(2):
                    i = V.bn_aggr(mv[r][:, j, :], st2[r][:, j, :])
                i.then_inc(s["aggr"], 1)

            def norm_x(B):
                r = B[1] % 2
                dve.wait_ge(s["ln_pow"], at(B, 1, 1))
                need(dve, s["xt_ps"], at(B, 1, -1))
                for j in range(2):
                    t = at(B, 2, j)
                    i = V.tensor_scalar(xh[r][:, j, :], x_sb[:, bass.ds(t, 1), :].rearrange("p o d -> p (o d)"), mv[r][:, j, 0:1],
                                        rstd[r][:, j:j + 1], ALU.subtract, ALU.mult)
                i.then_inc(s["ln_xh"], 1)

            def middle(B):
                r = B[1] % 2
                dve.wait_ge(s["hi"], at(B, 1, 1))
                need(dve, s["lo"], at(B, 1))
                V.scalar_tensor_tensor(rest[:].rearrange("p (a t) -> p a t", a=2), pA[:].rearrange("p (a t) -> p a t", a=2),
                                       QK_SCALE, parts[r][:, 0, :, :], ALU.mult, ALU.subtract).then_inc(s["rest"], 1)

            def m_reduce(B, u, banks=pM):
                r = B[1] % 2
                dve.wait_ge(s["m_ps"], at(B, 12, u + 1))
                if u == 0:
                    need(dve, s["mchain"], at(B, 3, -3))
                hh = u % 2
                if u < 8:
                    n, w, g0, blk = 2, 256, 2 * (u // 2), 1
                else:
                    n, w, g0, blk = 4, 128, 4 * ((u - 8) // 2), 0
                V.tensor_reduce(nmax[r][:, blk, hh, g0:g0 + n], banks[u % 2].rearrange("p (n w) -> p n w", w=w), AX.X, ALU.max,
                                negate=True).then_inc(s["m_neg"], 1)

            def m_split(B):
                r = B[1] % 2
                hi, mid, lo = (mparts[r][:, :, :, k, :].rearrange("p b a g -> p (b a) g") for k in range(3))
                nm = nmax[r][:].rearrange("p b a g -> p (b a) g")
                nr = nrest[:].rearrange("p b a g -> p (b a) g")
                dve.wait_ge(s["m_neg"], at(B, 12, 12))
                need(dve, s["mt_ps"], at(B, 1, -1))
                V.tensor_copy(hi, nm).then_inc(s["mchain"], 1)
                dve.wait_ge(s["mchain"], at(B, 3, 1))
                V.tensor_tensor(nr, nm, hi, ALU.subtract).then_inc(s["mchain"], 1)
                dve.wait_ge(s["mchain"], at(B, 3, 2))
                V.tensor_copy(mid, nr).then_inc(s["mchain"], 1)
                dve.wait_ge(s["mchain"], at(B, 3, 3))
                V.tensor_tensor(lo, nr, mid, ALU.subtract).then_inc(s["m_split"], 1)

            def norm_o(B, k):
                r = B[1] % 2
                v = pC[:].rearrange("p (j h w) -> p j h w", j=2, w=VW)
                dve.wait_ge(s["back_ps"], at(B, 2, k + 1))
                need(dve, s["o_nrm"], at(B, 2, k))
                V.reciprocal(rec[:], v[:, :, :, HD]).then_inc(s["o_rec"], 1)
                dve.wait_ge(s["o_rec"], at(B, 2, k + 1))
                if k == 0:
                    need(dve, s["ot_ps"], at(B, 1, -1))
                V.tensor_tensor(o_sb[r][:, :, 64 * k:64 * k + 64].rearrange("p j (h d) -> p j h d", d=HD), v[:, :, :, 0:HD],
                                rec[:].rearrange("p j (h o) -> p j h o", o=1).to_broadcast([P, 2, 8, HD]), ALU.mult).then_inc(s["o_nrm"], 1)

            def add_attn(B):
                dve.wait_ge(s["wo_ps"], at(B, 1, 1))
                xt = x_sb[:, tiles(B), :].rearrange("p a d -> p (a d)")
                V.tensor_tensor(xt, pC[:, 256:512], xt, ALU.add).then_inc(s["x_attn"], 1)

            start, tile, tiles_between = experts(0)
            start()
            tile(0, 0)
            half_probability(1)
            for t in range(1, 4):
                tile(0, t)
            tiles_between(4, EARLY)
            b0, b1, b2 = (0, 0), (0, 1), (0, 2)
            for t in range(EARLY, NS + 1):
                if t > EARLY:
                    tile(0, t - 1)
                if t == 25:
                    residual(b0)
                if t == 26:
                    residual(b1)
                if t == 27:
                    norm_x(b0)
                if t == 28:
                    norm_x(b1)
                    residual(b2)
                if t == 30:
                    middle(b0)
                if t == 31:
                    norm_x(b2)
                if t == 32:
                    middle(b1)
                if 36 <= t < 42:
                    m_reduce(b0, 2 * (t - 36), (pO[:], pC[:]))
                    m_reduce(b0, 2 * (t - 36) + 1, (pO[:], pC[:]))
                if t == 42:
                    m_split(b0)

            def r_stats(B):
                r = B[1] % 2
                dve.wait_ge(s["x_attn"], at(B, 1, 1))
                alone(dve)
                for j in range(2):
                    i = V.bn_stats(st3[r][:, j, :], x_sb[:, bass.ds(at(B, 2, j), 1), :].rearrange("p o d -> p (o d)"))
                i.then_inc(s["r_stats"], 1)
                dve.wait_ge(s["r_stats"], at(B, 1, 1))
                need(dve, s["r_veps"], at(B, 1, -1))
                alone(dve)
                for j in range(2):
                    i = V.bn_aggr(mv3[r][:, j, :], st3[r][:, j, :])
                i.then_inc(s["r_aggr"], 1)

            def r_norm(B):
                r = B[1] % 2
                dve.wait_ge(s["r_pow"], at(B, 1, 1))
                need(dve, s["r_tps"], at(B, 1, -1))
                need(dve, s["r_copied"], at(B, 1, -1))
                for j in range(2):
                    i = V.tensor_scalar(xr[r][:, j, :], x_sb[:, bass.ds(at(B, 2, j), 1), :].rearrange("p o d -> p (o d)"), mv3[r][:, j, 0:1],
                                        rstd3[r][:, j:j + 1], ALU.subtract, ALU.mult)
                i.then_inc(s["r_xh"], 1)

            def r_keep_logits(B):
                dve.wait_ge(s["r_lps"], at(B, 1, 1))
                V.tensor_copy(lg_all[:, tiles(B), :], pA[:, 256:256 + 2 * NE].rearrange("p (a e) -> p a e", e=NE)).then_inc(s["r_lg"], 1)

            def dve_step(B):
                if has(B, 1):
                    m_reduce(nxt(B, 1), 0)
                    m_reduce(nxt(B, 1), 1)
                if has(B, -2):
                    norm_o(nxt(B, -2), 1)
                if has(B, 1):
                    m_reduce(nxt(B, 1), 2)
                    m_reduce(nxt(B, 1), 3)
                if has(B, 2):
                    middle(nxt(B, 2))
                if has(B, 1):
                    m_reduce(nxt(B, 1), 4)
                    m_reduce(nxt(B, 1), 5)
                    m_reduce(nxt(B, 1), 6)
                    m_reduce(nxt(B, 1), 7)
                if has(B, -2):
                    add_attn(nxt(B, -2))
                if has(B, 1):
                    m_reduce(nxt(B, 1), 8)
                    m_reduce(nxt(B, 1), 9)
                    m_reduce(nxt(B, 1), 10)
                    m_reduce(nxt(B, 1), 11)
                    m_split(nxt(B, 1))
                if has(B, 3):
                    residual(nxt(B, 3))
                if has(B, -2):
                    r_stats(nxt(B, -2))
                if is_step(B, 13):
                    choose(2)
                if is_step(B, 14):
                    experts_of(2)
                    half_probability(2)
                if has(B, 3):
                    norm_x(nxt(B, 3))
                if has(B, -1):
                    norm_o(nxt(B, -1), 0)
                if has(B, -2):
                    r_norm(nxt(B, -2))
                if has(B, -3):
                    r_keep_logits(nxt(B, -3))
                if is_step(B, 13):
                    places(2, pM[0])

            steps(dve, dve_step)
            start, tile, tiles_between = experts(1)
            b14, b15 = (0, NB - 2), (0, NB - 1)
            norm_o(b14, 1)
            start()
            tile(0, 0)
            add_attn(b14)
            r_stats(b14)
            norm_o(b15, 0)
            tile(0, 1)
            r_keep_logits((0, NB - 3))
            r_norm(b14)
            tile(0, 2)
            norm_o(b15, 1)
            tile(0, 3)
            tile(0, 4)
            add_attn(b15)
            r_stats(b15)
            tile(0, 5)
            r_keep_logits(b14)
            r_norm(b15)
            tile(0, 6)
            tile(0, 7)
            r_keep_logits(b15)
            choose(3)
            tile(0, 8)
            places(3, pA)
            tile(0, 9)
            experts_of(3)
            tile(0, 10)
            half_probability(3)
            tile(0, 11)
            tiles_between(12, 40)
            for t in range(40, NS):
                tile(0, t)
            for k in range(GT[1][1] // 4):
                dve.wait_ge(fin_y[k], 64)
                for t in range(T0[1][1] + 4 * k, T0[1][1] + 4 * k + 4):
                    i = V.scalar_tensor_tensor(x_sb[:, t, :], xh_all[:, t, :], pmax[:, t:t + 1], x_sb[:, t, :], ALU.mult, ALU.add)
                i.then_inc(s["fin_x"], 1)


def kernel(L0_attn_x, L0_attn_Wq, L0_attn_Wk, L0_attn_Wv, L0_attn_Wo, L0_ffn_Wr, L0_ffn_W1, L0_ffn_b1, L0_ffn_W2, L0_ffn_b2):
    import ml_dtypes
    import numpy as np
    import concourse.bacc as bacc
    from concourse.bass_utils import run_bass_kernel_spmd

    f32 = np.float32
    bf16 = ml_dtypes.bfloat16
    c = np.ascontiguousarray

    w1b = np.concatenate([L0_ffn_W1, L0_ffn_b1.reshape(NE, FC, P).transpose(0, 2, 1),
                          np.broadcast_to(L0_ffn_b2[:, None, :], (NE, P, D))], axis=2)
    order = np.array([(2 * g + hh) * HD + d for hh in range(2) for d in range(HD) for g in range(8)])

    cf = np.zeros((P, C_END), f32)
    cf[:, 0:P] = np.eye(P)
    cf[:, C_STEPS:C_STEPS + TM] = np.arange(TM) * P
    for n, w in enumerate(GROUPS):
        cf[:, C_KEEP[n]:C_KEEP[n] + NE * w] = np.arange(NE * w) % w != 0
    cf[:, C_RANK:C_RANK + NE] = NE - np.arange(NE)
    cf[:, C_IDS:C_IDS + SM] = np.arange(SM)
    cf[:, C_ONES:C_ONES + NE] = 1
    cf[:, C_HALF:C_END] = -0.5
    i = np.arange(P)
    cb = np.zeros((P, 640), f32)
    cb[:, 0:128] = np.eye(P)
    cb[:, 128:256] = i[:, None] < i[None, :]
    cb[:, 256:384] = 1
    cb[:, 384:512] = np.where(i[None, :] > i[:, None], -1e30, 0)
    cb[:, 512:640] = np.where(i[:, None] > i[None, :], -1e30, 0)

    def three(a):
        hi = a.astype(bf16)
        mid = (a - hi.astype(np.float64)).astype(bf16)
        lo = (a - hi.astype(np.float64) - mid.astype(np.float64)).astype(bf16)
        return hi, mid, lo

    base = 2.0 ** (-8.0 / H)
    slopes = np.array([base ** n for n in range(1, H + 1)], dtype=f32).astype(np.float64)
    qconst = np.ones((2, 6, 8, 256), bf16)
    kconst = np.ones((2, 9, 8, 256), bf16)
    for hh in range(2):
        for g in range(8):
            bias = three(slopes[2 * g + hh] * (np.arange(256) - 128.0))
            for n in range(3):
                kconst[hh, n, g] = bias[n]
                qconst[hh, 3 + n, g] = -bias[n]

    arrays = {
        "x": c(L0_attn_x.reshape(NT * P, D)), "w1b": c(w1b), "w2": c(L0_ffn_W2),
        "wr": c(L0_ffn_Wr),
        "wq": c(L0_attn_Wq[order].T), "wk": c(L0_attn_Wk[order].T), "wv": c(L0_attn_Wv.T), "wo": c(L0_attn_Wo.T),
        "cf": cf, "cb": cb.astype(bf16), "qconst": qconst, "kconst": kconst,
    }
    nc = bacc.Bacc("TRN2", target_bir_lowering=False, num_devices=1)
    args = []
    for name, a in arrays.items():
        args.append(nc.dram_tensor(f"in_{name}", a.shape, mybir.dt.from_np(a.dtype), kind="ExternalInput").ap())
    out = nc.dram_tensor("out", (NT * P, D), F32, kind="ExternalOutput").ap()
    build(nc, *args, out)
    r = run_bass_kernel_spmd(nc, [{f"in_{n}": a for n, a in arrays.items()}], core_ids=[0])
    return r.results[0]["out"].reshape(NB, 256, D)
```
